# Optimizing a Trainium2 kernel written in Bass

```python
import numpy as np
import jax
import jax.numpy as jnp

def _softmax(x, axis=-1):
    return jax.nn.softmax(x, axis=axis)

def _gelu(x):
    return jax.nn.gelu(x, approximate=True)

def _silu(x):
    return jax.nn.silu(x)

def _sigmoid(x):
    return jax.nn.sigmoid(x)

def _layernorm(x, axis=-1, eps=1e-05):
    m = jnp.mean(x, axis=axis, keepdims=True)
    v = jnp.var(x, axis=axis, keepdims=True)
    return (x - m) / jnp.sqrt(v + eps)

def _scatter_add(tgt, idx, src, axis=0):
    return tgt.at[idx].add(src)

def _segment_sum(src, seg, n):
    return jax.ops.segment_sum(src, seg, n)
kernel_name = 'mk_gnn_preln_d2_gnn_r8_d4853f'

def setup_inputs(seed: int=0):
    np.random.seed(seed)
    _w = jnp.asarray

    def _rec_inputs():
        import jax
        import jax.numpy as jnp
        _gk = jax.random.key(seed)
        x = -0.0003713 + 1 * jax.random.normal(jax.random.fold_in(_gk, 1), (12500, 128), jnp.float32)
        src = jax.random.randint(jax.random.fold_in(_gk, 2), (400000,), 0, 12500, jnp.int32)
        dst = jax.random.randint(jax.random.fold_in(_gk, 3), (400000,), 0, 12500, jnp.int32)
        _o = jnp.argsort(dst, stable=True)
        src = src[_o]
        dst = dst[_o]
        edge_type_201 = jax.random.randint(jax.random.fold_in(_gk, 13), (400000,), 0, 201, jnp.int32)
        edge_type_8 = jax.random.randint(jax.random.fold_in(_gk, 14), (400000,), 0, 8, jnp.int32)
        return (x, src, dst, edge_type_201, edge_type_8)
    x, src, dst, edge_type_201, edge_type_8 = _rec_inputs()

    def _L0_gnn_setup():
        import jax, jax.numpy as jnp
        import numpy as np
        N_ENT = 12500

        def _rgcn_layer(x, W, SW, b, src, dst, rel):
            xt = jnp.einsum('nd,rde->rne', x, W)
            msg = xt[rel, src]
            agg = jax.ops.segment_sum(msg, dst, num_segments=x.shape[0])
            return jax.nn.relu(agg + x @ SW + b)
        key = jax.random.key(seed)
        ks = jax.random.split(key, 8)
        d, R, E = (128, 8, 75000)
        scale = 1.0 / np.sqrt(d)
        return {'entity_emb': jax.random.normal(ks[0], (N_ENT, d), dtype=jnp.float32), 'w1': jax.random.normal(ks[1], (R, d, d), dtype=jnp.float32) * scale, 'sl1': jax.random.normal(ks[2], (d, d), dtype=jnp.float32) * scale, 'b1': jnp.zeros((d,), dtype=jnp.float32), 'w2': jax.random.normal(ks[3], (R, d, d), dtype=jnp.float32) * scale, 'sl2': jax.random.normal(ks[4], (d, d), dtype=jnp.float32) * scale, 'b2': jnp.zeros((d,), dtype=jnp.float32), 'edge_index': jax.random.randint(ks[5], (2, E), 0, N_ENT, dtype=jnp.int64), 'edge_type': jax.random.randint(ks[6], (E,), 0, R, dtype=jnp.int64)}
    _L0_gnn_all = _L0_gnn_setup()
    _L0_gnn_in = {k: v for k, v in _L0_gnn_all.items() if k in ('w1', 'sl1', 'b1', 'w2', 'sl2', 'b2')}
    del _L0_gnn_all

    def _L1_gnn_setup():
        import jax, jax.numpy as jnp
        import numpy as np
        import math
        N = 12500
        IN = 128
        OUT = 128
        R = 200
        T = 62500
        E = 2 * T + N
        key = jax.random.key(seed)
        k = jax.random.split(key, 8)
        stdv = 1.0 / math.sqrt(OUT)
        src1 = jax.random.randint(k[0], (T,), 0, N, dtype=jnp.int32)
        dst1 = jax.random.randint(k[1], (T,), 0, N, dtype=jnp.int32)
        loops = jnp.arange(N, dtype=jnp.int32)
        src = jnp.concatenate([src1, dst1, loops])
        dst = jnp.concatenate([dst1, src1, loops])
        et1 = jax.random.randint(k[2], (T,), 1, R + 1, dtype=jnp.int32)
        et2 = jax.random.randint(k[3], (T,), 1, R + 1, dtype=jnp.int32)
        et_loop = jnp.full((N,), R, dtype=jnp.int32)
        all_edge_type = jnp.concatenate([et1, et2, et_loop])
        x = jax.random.normal(k[4], (N, IN), dtype=jnp.float32)
        weight = jax.random.uniform(k[5], (IN, OUT), jnp.float32, -stdv, stdv)
        bias = jax.random.uniform(k[6], (OUT,), jnp.float32, -stdv, stdv)
        alpha = jax.random.normal(k[7], (R + 1, 1), dtype=jnp.float32)
        alpha = alpha.at[0].set(0.0)
        return {'input': x, 'all_edge_type': all_edge_type, 'src': src, 'dst': dst, 'weight': weight, 'alpha': alpha, 'bias': bias}
    _L1_gnn_all = _L1_gnn_setup()
    _L1_gnn_in = {k: v for k, v in _L1_gnn_all.items() if k in ('weight', 'alpha', 'bias')}
    del _L1_gnn_all
    return {'x': x, 'src': src, 'dst': dst, 'edge_type_201': edge_type_201, 'edge_type_8': edge_type_8, 'L0_gnn_w1': _L0_gnn_in['w1'], 'L0_gnn_sl1': _L0_gnn_in['sl1'], 'L0_gnn_b1': _L0_gnn_in['b1'], 'L0_gnn_w2': _L0_gnn_in['w2'], 'L0_gnn_sl2': _L0_gnn_in['sl2'], 'L0_gnn_b2': _L0_gnn_in['b2'], 'L1_gnn_weight': _L1_gnn_in['weight'], 'L1_gnn_alpha': _L1_gnn_in['alpha'], 'L1_gnn_bias': _L1_gnn_in['bias']}

def reference(x, src, dst, edge_type_201, edge_type_8, L0_gnn_w1, L0_gnn_sl1, L0_gnn_b1, L0_gnn_w2, L0_gnn_sl2, L0_gnn_b2, L1_gnn_weight, L1_gnn_alpha, L1_gnn_bias):
    import jax
    import jax.numpy as jnp

    def _L0_gnn_ref(entity_emb, w1, sl1, b1, w2, sl2, b2, edge_index, edge_type):
        import jax, jax.numpy as jnp
        import numpy as np
        N_ENT = 12500

        def _rgcn_layer(x, W, SW, b, src, dst, rel):
            xt = jnp.einsum('nd,rde->rne', x, W)
            msg = xt[rel, src]
            agg = jax.ops.segment_sum(msg, dst, num_segments=x.shape[0])
            return jax.nn.relu(agg + x @ SW + b)
        src, dst = (edge_index[0], edge_index[1])
        x = _rgcn_layer(entity_emb, w1, sl1, b1, src, dst, edge_type)
        x = _rgcn_layer(x, w2, sl2, b2, src, dst, edge_type)
        return x

    def _L1_gnn_ref(input, all_edge_type, src, dst, weight, alpha, bias):
        import jax, jax.numpy as jnp
        import numpy as np
        import math
        N = 12500
        IN = 128
        OUT = 128
        R = 200
        T = 62500
        E = 2 * T + N
        n = input.shape[0]
        e = all_edge_type.shape[0]
        t = (e - n) // 2
        tbl = alpha.at[0].set(0.0)
        feats = input @ weight
        t_et = jnp.concatenate([all_edge_type[t:2 * t], all_edge_type[:t], all_edge_type[-n:]])
        alp = tbl[all_edge_type] + tbl[t_et]
        msg = feats[src] * alp
        out = jax.ops.segment_sum(msg, dst, num_segments=n)
        return out + bias
    edge_index = jnp.stack([src, dst])
    h = jnp.maximum(_layernorm(x, axis=-1), 0.0)
    x = x + _L0_gnn_ref(h, L0_gnn_w1, L0_gnn_sl1, L0_gnn_b1, L0_gnn_w2, L0_gnn_sl2, L0_gnn_b2, edge_index, edge_type_8)
    h = jnp.maximum(_layernorm(x, axis=-1), 0.0)
    x = x + _L1_gnn_ref(h, edge_type_201, src, dst, L1_gnn_weight, L1_gnn_alpha, L1_gnn_bias)
    return x

_drawn_inputs = setup_inputs


def setup_inputs(seed=0):
    import zlib

    import numpy as np

    out = dict(_drawn_inputs(seed))
    spreads = {'L0_gnn_b1': (0.0, 0.412), 'L0_gnn_b2': (0.0, 2.0)}
    factors = {'L1_gnn_bias': 30.136}
    for name, (base, spread) in spreads.items():
        noise = np.random.default_rng([zlib.crc32(name.encode()), seed]).standard_normal(out[name].shape)
        drawn = base * np.exp(spread * noise) if base else spread * noise
        out[name] = jnp.asarray(drawn.astype(out[name].dtype))
    for name, factor in factors.items():
        out[name] = (out[name] * factor).astype(out[name].dtype)
    return out
```

```python
from contextlib import ExitStack

import concourse.bass as bass
from concourse import mybir

P = 128
WIN = 256
BLOCK = 19
LOOKAHEAD = 2
RING = 4
EPS = 1e-5


def split(n, most=8192):
    for unit in (16, 10, 5, 2, 1):
        for rows in range(unit, n + 1, unit):
            if n % rows == 0 and n // rows <= most:
                return rows, n // rows


def build(nc, x, src, dst, etype, rel, w1, sl1, b1, w2, sl2, b2, weight, alpha, bias, out):
    fp32, i32, i16 = mybir.dt.float32, mybir.dt.int32, mybir.dt.int16
    ALU = mybir.AluOpType
    ACT = mybir.ActivationFunctionType

    NODES, D = x.shape
    EDGES = src.shape[0]
    R = w1.shape[0]
    TYPES = alpha.shape[0]
    TILES = -(-NODES // P)
    TAIL = NODES - (TILES - 1) * P
    CHUNKS = EDGES // P
    WINS = -(-NODES // WIN)
    VISITS = -(-(CHUNKS + WINS - 1) // BLOCK) * BLOCK
    BLOCKS = VISITS // BLOCK
    VT = -(-VISITS // P)
    HALF = (EDGES - NODES) // 2
    COLS = TILES * P
    assert TILES % 2 == 0 and TILES >= 4 and D == P and EDGES % P == 0 and VT >= 3 and WINS * WIN >= NODES
    GROUPS = [(g, min(5, BLOCK - g)) for g in range(0, BLOCK, 5)]
    NG = len(GROUPS)
    LR = max(r for r in range(1, P + 1) if CHUNKS % r == 0)
    LC = CHUNKS // LR
    TAB = R * D
    HT = TAB // 2

    xt1 = nc.dram_tensor("xt1", (COLS * R, D), fp32, kind="Internal").ap()
    xt2 = nc.dram_tensor("xt2", (COLS * R, D), fp32, kind="Internal").ap()
    h2_d = nc.dram_tensor("h2_d", (COLS, D), fp32, kind="Internal").ap()
    tet_d = nc.dram_tensor("tet_d", (EDGES,), i32, kind="Internal").ap()
    last_d = nc.dram_tensor("last_d", (CHUNKS,), i32, kind="Internal").ap()
    base_d = nc.dram_tensor("base_d", (VT * P,), i32, kind="Internal").ap()

    with ExitStack() as ctx:
        def sb(name, shape, dt=fp32):
            return ctx.enter_context(nc.sbuf_tensor(name, shape, dt))

        def sem(name):
            return ctx.enter_context(nc.semaphore(name))

        x_res = sb("x_res", [P, TILES, D])
        agg = sb("agg", [P, COLS])
        index_t = sb("index_t", [P, VT * P], i32)
        place_t = sb("place_t", [P, VT * P])
        type_t = sb("type_t", [P, VT * P])
        rtype_t = sb("rtype_t", [P, VT * P])
        base_t = sb("base_t", [1, VT * P], i32)
        iota_i = sb("iota_i", [P, max(WIN, TYPES)], i32)
        iota_f = sb("iota_f", [P, max(WIN, TYPES)])
        row_i = sb("row_i", [P, 1], i32)
        row_f = sb("row_f", [P, 1])
        visit_i = sb("visit_i", [P, VT], i32)
        visit_f = sb("visit_f", [P, VT])
        win_first = sb("win_first", [P, 1])
        ident = sb("ident", [P, P])
        ones = sb("ones", [P, P])
        eps_c = sb("eps_c", [P, 1])
        w_sb = sb("w_sb", [P, R, D])
        sl_sb = sb("sl_sb", [P, D])
        b_col = sb("b_col", [P, 1])
        weight_sb = sb("weight_sb", [P, D])
        bias_sb = sb("bias_sb", [P, D])
        alpha_sb = sb("alpha_sb", [P, TYPES])
        last_sb = sb("last_sb", [P, LC], i32)
        start_c = sb("start_c", [P, 1])
        start_v = sb("start_v", [P, 1])
        start_d = sb("start_d", [P, WINS])
        start_b = sb("start_b", [P, WINS])
        count_o = sb("count_o", [P, WINS])
        win_v = sb("win_v", [P, VT])
        chunk_v = sb("chunk_v", [P, VT])
        chunk_i = sb("chunk_i", [P, VT], i32)
        first_v = sb("first_v", [P, VT])
        base_v = sb("base_v", [P, VT])
        base_r = sb("base_r", [P, P], i32)
        chunk_s = sb("chunk_s", [P, 2], i32)
        stats = sb("stats", [P, TILES, 6])
        mean = sb("mean", [P, TILES])
        gap = sb("gap", [P, TILES])
        var = sb("var", [P, TILES])
        std = sb("std", [P, TILES])
        rstd = sb("rstd", [P, TILES])
        nmr = sb("nmr", [P, TILES])
        hn = sb("hn", [P, 2, P])
        hs = sb("hs", [P, 2, P])
        xts = sb("xts", [P, 2, TAB])
        index_s = sb("index_s", [P, BLOCK], i32)
        msgs = sb("msgs", [P, BLOCK, D])
        raw = msgs[:, 0:10, :].bitcast(i32).rearrange("p (s a) e -> p s a e", s=2)
        conv = msgs[:, 10:18, :].rearrange("p (s a) e -> p s a e", s=2)
        onehot = sb("onehot", [P, RING, WIN])
        place_s = sb("place_s", [P, BLOCK])
        type_s = sb("type_s", [P, BLOCK])
        alpha_s = sb("alpha_s", [P, BLOCK])
        look_o = sb("look_o", [P, RING, TYPES])
        bank = [ctx.enter_context(nc.psum_tensor(f"bank{i}", [P, 512], fp32)) for i in range(8)]

        last_b = index_t[0:WINS, 0:CHUNKS]
        last_f = place_t[0:WINS, 0:CHUNKS]
        below_o = type_t[0:WINS, 0:CHUNKS]

        s_x = sem("x_loaded")
        s_dst = sem("last_loaded")
        s_last = sem("last_stored")
        s_lastb = sem("last_broadcast")
        s_tet = sem("reverse_types_stored")
        s_w = sem("weights_loaded")
        s_w2 = sem("second_weights_loaded")
        s_zero = sem("tail_tile_cleared")
        s_iota = sem("iotas_written")
        s_const = sem("constants_written")
        s_dve = sem("vector_step_done")
        s_diag = sem("window_starts_on_diagonal")
        s_spread = sem("window_starts_broadcast")
        s_chunks = sem("visit_chunks_written")
        s_baseT = sem("bases_transposed")
        s_baser = sem("base_rows_written")
        s_based = sem("bases_stored")
        s_base = sem("bases_loaded")
        s_cs = sem("chunk_slot_written")
        s_raw = [sem("raw_rows_gathered_0"), sem("raw_rows_gathered_1")]
        s_conv = sem("raw_rows_converted")
        s_tabT = sem("table_transposed")
        s_tab = sem("table_written")
        s_bn = sem("tile_stats_done")
        s_var = sem("variances_ready")
        s_std = sem("std_ready")
        s_norm = sem("norm_factors_ready")
        s_hn = sem("normed_tile_ready")
        s_hT = sem("normed_tile_transposed")
        s_hs = sem("stationary_tile_ready")
        s_xf = sem("tile_transformed")
        s_eva = sem("left_half_evacuated")
        s_evd = sem("right_half_evacuated")
        s_ag = sem("self_term_in_agg")
        s_xts = [sem("tile_rows_stored_0"), sem("tile_rows_stored_1")]
        s_idx = sem("index_group_ready")
        s_g = [sem(f"group_gathered_{g}") for g in range(NG)]
        s_oh = sem("onehot_ready")
        s_mm = sem("product_done")
        s_add = sem("product_added")
        s_place = sem("places_and_types_ready")
        s_look = sem("alpha_looked_up")
        s_alpha = sem("alphas_kept")
        s_wgt = sem("edge_weights_ready")
        s_rl = sem("relu_tile_ready")
        s_rT = sem("relu_tile_transposed")
        s_rx = sem("residual_added")
        s_h2 = sem("second_norm_tile_ready")
        s_h2b = sem("bias_added")
        s_h2d = [sem("second_norm_stored_0"), sem("second_norm_stored_1")]
        s_fc = sem("final_stationary_ready")
        s_fm = sem("final_product_done")
        s_fa = sem("final_added")
        s_out = sem("output_stored")

        block = ctx.enter_context(nc.Block())

        def need(eng, s, value):
            if not isinstance(value, int) or value > 0:
                eng.wait_ge(s, value)

        def over_tiles(eng, step):
            step(0, 0)
            step(1, 1)
            with eng.Fori(1, TILES // 2) as i:
                step(i * 2, 0)
                step(i * 2 + 1, 1)

        def lagged_tiles(eng, ahead, behind):
            ahead(0, 0)
            ahead(1, 1)
            behind(0, 0)
            ahead(2, 0)
            behind(1, 1)
            with eng.Fori(1, TILES // 2 - 1) as i:
                ahead(i * 2 + 1, 1)
                behind(i * 2, 0)
                ahead(i * 2 + 2, 0)
                behind(i * 2 + 1, 1)
            ahead(TILES - 1, 1)
            behind(TILES - 2, 0)
            behind(TILES - 1, 1)

        def over_visit_tiles(eng, step):
            step(0, 0)
            step(1, 1)
            if VT >= 4:
                with eng.Fori(1, VT // 2) as i:
                    step(i * 2, 0)
                    step(i * 2 + 1, 1)
            if VT % 2:
                step(VT - 1, 0)

        def over_blocks(eng, layer, step):
            step(0, layer * BLOCKS)
            with eng.Fori(1, BLOCKS) as j:
                step(j, j + layer * BLOCKS)

        def cols(t, width=P):
            return bass.ds(t * width, width)

        def half16(t, s):
            return t * 8 + (-8 * s)

        def stored(eng, layer, t, s):
            eng.wait_ge(s_xts[s], t * 8 + (8 * layer * TILES - 8 * s))

        @block.sync
        def _(sp):
            with nc.allow_non_contiguous_dma("last destination of each chunk, biases as columns"):
                sp.dma_start(last_sb[0:LR, 0:LC],
                             dst.rearrange("(a b p) -> a b p", a=LR, p=P)[:, :, P - 1]).then_inc(s_dst, 16)
            cuts = [(TILES - 1) * q // 4 for q in range(5)]
            for a, b in zip(cuts, cuts[1:]):
                sp.dma_start(x_res[:, a:b, :], x[a * P:b * P, :].rearrange("(t p) d -> p t d", p=P)).then_inc(s_x, 16)
            sp.wait_ge(s_zero, 1)
            sp.dma_start(x_res[0:TAIL, TILES - 1, :], x[(TILES - 1) * P:NODES, :]).then_inc(s_x, 16)
            sp.wait_ge(s_dst, 16)
            sp.dma_start(last_d.rearrange("(a b) -> a b", a=LR), last_sb[0:LR, 0:LC]).then_inc(s_last, 16)
            for to, frm, n in ((0, HALF, HALF), (HALF, 0, HALF), (2 * HALF, 2 * HALF, NODES)):
                a, _b = split(n)
                sp.dma_start(tet_d[to:to + n].rearrange("(a b) -> a b", a=a),
                             etype[frm:frm + n].rearrange("(a b) -> a b", a=a)).then_inc(s_tet, 16)
            sp.wait_ge(s_last, 16)
            sp.dma_start(last_b, last_d.partition_broadcast(WINS)).then_inc(s_lastb, 16)
            sp.dma_start(w_sb[:, :, :], w1.rearrange("r d e -> d r e")).then_inc(s_w, 16)
            sp.dma_start(sl_sb[:, :], sl1).then_inc(s_w, 16)
            sp.dma_start(weight_sb[:, :], weight).then_inc(s_w, 16)
            with nc.allow_non_contiguous_dma("biases as columns"):
                sp.dma_start(b_col[:, :], b1.rearrange("(d o) -> d o", o=1)).then_inc(s_w, 16)
                sp.dma_start(bias_sb[:, :], bias.partition_broadcast(P)).then_inc(s_w, 16)
                sp.dma_start(alpha_sb[:, :], alpha.rearrange("r o -> (r o)").partition_broadcast(P)).then_inc(s_w, 16)
            sp.wait_ge(s_baser, 1)
            sp.dma_start(base_d.rearrange("(t p) -> t p", p=P), base_r[0:VT, :]).then_inc(s_based, 16)
            sp.wait_ge(s_based, 16)
            sp.dma_start(base_t[:, :], base_d.rearrange("(o n) -> o n", o=1)).then_inc(s_base, 16)

            def store_rows(layer, table):
                def step(t, s):
                    done = t + (layer * TILES + 1)
                    need(sp, s_eva, done)
                    need(sp, s_evd, done)
                    rows = table.rearrange("(n r) d -> n (r d)", r=R)
                    sp.dma_start(rows[cols(t), :], xts[:, s, :]).then_inc(s_xts[s], 16)
                over_tiles(sp, step)

            store_rows(0, xt1)
            sp.wait_ge(s_xf, TILES)
            sp.wait_ge(s_ag, TILES)
            sp.dma_start(w_sb[:, :, :], w2.rearrange("r d e -> d r e")).then_inc(s_w2, 16)
            sp.dma_start(sl_sb[:, :], sl2).then_inc(s_w2, 16)
            with nc.allow_non_contiguous_dma("biases as columns"):
                sp.dma_start(b_col[:, :], b2.rearrange("(d o) -> d o", o=1)).then_inc(s_w2, 16)
            store_rows(1, xt2)

            def store_h2(t, s):
                sp.wait_ge(s_h2, t + 1)
                sp.dma_start(h2_d[cols(t), :], hn[:, s, :]).then_inc(s_h2d[s], 16)
            over_tiles(sp, store_h2)

            for a, b in zip(cuts, cuts[1:]):
                sp.wait_ge(s_fa, b)
                sp.dma_start(out[a * P:b * P, :].rearrange("(t p) d -> p t d", p=P), x_res[:, a:b, :]).then_inc(s_out, 16)
            sp.wait_ge(s_fa, TILES)
            sp.dma_start(out[(TILES - 1) * P:NODES, :], x_res[0:TAIL, TILES - 1, :]).then_inc(s_out, 16)
            sp.wait_ge(s_out, 80)

        @block.gpsimd
        def _(pool):
            nc.gpsimd.iota(iota_i[:, :], pattern=[[1, max(WIN, TYPES)]], base=0, channel_multiplier=0).then_inc(s_iota, 1)
            nc.gpsimd.iota(row_i[:, :], pattern=[[0, 1]], base=0, channel_multiplier=1).then_inc(s_iota, 1)
            nc.gpsimd.iota(visit_i[:, :], pattern=[[P, VT]], base=0, channel_multiplier=1).then_inc(s_iota, 1)

            arrays = [a.rearrange("(c p) -> c p", p=P) for a in (dst, src, rel, etype, tet_d)]
            pool.wait_ge(s_tet, 48)

            def table_rows(t, s):
                need(pool, s_cs, t + 1)
                need(pool, s_conv, t + (-1))
                pool.nop(nofuse=True)
                for a in range(5):
                    pool.indirect_dma_start(out=raw[:, s, a, :], out_offset=None, in_=arrays[a],
                                            in_offset=bass.IndirectOffsetOnAxis(ap=chunk_s[:, s:s + 1], axis=0)
                                            ).then_inc(s_raw[s], 16)
            over_visit_tiles(pool, table_rows)

            def gather_layer(layer, table):
                def step(j, n):
                    for g, (first, size) in enumerate(GROUPS):
                        pool.wait_ge(s_idx, n * NG + (g + 1))
                        need(pool, s_mm, n * BLOCK + (first + size - BLOCK))
                        pool.nop(nofuse=True)
                        for k in range(first, first + size):
                            pool.indirect_dma_start(out=msgs[:, k, :], out_offset=None, in_=table,
                                                    in_offset=bass.IndirectOffsetOnAxis(ap=index_s[:, k:k + 1], axis=0)
                                                    ).then_inc(s_g[g], 16)
                over_blocks(pool, layer, step)

            for layer, table in ((0, xt1), (1, xt2)):
                for s in range(2):
                    pool.wait_ge(s_xts[s], 16 * (layer + 1) * (TILES // 2))
                gather_layer(layer, table)
            for s in range(2):
                pool.wait_ge(s_h2d[s], 16 * (TILES // 2))
            gather_layer(2, h2_d)

        @block.scalar
        def _(act):
            act.wait_ge(s_chunks, 1)

            def chunk_slot(t, s):
                need(act, s_raw[s], t * 40 + (-40 * s))
                nc.scalar.copy(chunk_s[:, s:s + 1], chunk_i[:, bass.ds(t, 1)]).then_inc(s_cs, 1)

            def table_out(t, s):
                act.wait_ge(s_tabT, t + 1)
                for a, tab in enumerate((place_t, index_t, type_t, rtype_t)):
                    last = nc.scalar.copy(tab[:, cols(t)], bank[s][:, a * P:(a + 1) * P])
                last.then_inc(s_tab, 1)
            chunk_slot(0, 0)
            chunk_slot(1, 1)
            table_out(0, 0)
            if VT >= 4:
                with act.Fori(1, VT // 2) as i:
                    chunk_slot(i * 2, 0)
                    table_out(i * 2 + (-1), 1)
                    chunk_slot(i * 2 + 1, 1)
                    table_out(i * 2, 0)
            if VT % 2:
                chunk_slot(VT - 1, 0)
                table_out(VT - 2, 1)
                table_out(VT - 1, 0)
            else:
                table_out(VT - 1, 1)

            act.wait_ge(s_var, 1)
            act.wait_ge(s_const, 1)
            nc.scalar.activation(std[:, :], var[:, :], ACT.Sqrt, bias=eps_c[:, 0:1]).then_inc(s_std, 1)
            act.wait_ge(s_norm, 1)

            def norm_tile(t, s):
                need(act, s_hT, t + (-1))
                nc.scalar.activation(hn[:, s, :], x_res[:, bass.ds(t, 1), :].rearrange("p o d -> p (o d)"), ACT.Relu,
                                     bias=nmr[:, bass.ds(t, 1)], scale=rstd[:, bass.ds(t, 1)]).then_inc(s_hn, 1)

            def relu_tile(t, s):
                need(act, s_xf, t + (TILES - 1))
                nc.scalar.activation(hs[:, s, :], agg[:, cols(t)], ACT.Relu).then_inc(s_hs, 1)

            def evac(layer):
                def step(t, s):
                    act.wait_ge(s_xf, t + (layer * TILES + 1))
                    if layer or not isinstance(t, int) or t >= 2:
                        stored(act, layer, t, s)
                    nc.scalar.copy(xts[:, s, 0:HT], bank[2 * s][:, 0:HT]).then_inc(s_eva, 1)
                return step

            lagged_tiles(act, norm_tile, evac(0))

            def indices(layer, types=None):
                def keep(j, n):
                    act.wait_ge(s_look, n * BLOCK + BLOCK)
                    nc.scalar.copy(types[:, bass.ds(j * BLOCK, BLOCK)], alpha_s[:, :]).then_inc(s_alpha, 1)

                def step(j, n):
                    for g, (first, size) in enumerate(GROUPS):
                        slots = slice(first, first + size)
                        columns = bass.ds(j * BLOCK + first, size)
                        need(act, s_g[g], n * (16 * size))
                        nc.scalar.copy(index_s[:, slots], index_t[:, columns]).then_inc(s_idx, 1)
                        need(act, s_add, n * BLOCK + (first + size - BLOCK))
                        nc.scalar.copy(place_s[:, slots], place_t[:, columns])
                        nc.scalar.copy(type_s[:, slots], (type_t if types is None else types)[:, columns]).then_inc(s_place, 1)
                        if g == NG - 1 and types is not None and not (isinstance(j, int) and j == 0):
                            keep(j + (-1), n + (-1))
                over_blocks(act, layer, step)
                if types is not None:
                    keep(BLOCKS - 1, (layer + 1) * BLOCKS - 1)

            indices(0, type_t)
            act.wait_ge(s_add, VISITS)
            lagged_tiles(act, relu_tile, evac(1))
            indices(1, rtype_t)

            act.wait_ge(s_add, 2 * VISITS)

            def relu_out(t, s):
                need(act, s_rT, t + (-1))
                nc.scalar.activation(hs[:, s, :], agg[:, cols(t)], ACT.Relu).then_inc(s_rl, 1)
            over_tiles(act, relu_out)

            act.wait_ge(s_var, 2)
            nc.scalar.activation(std[:, :], var[:, :], ACT.Sqrt, bias=eps_c[:, 0:1]).then_inc(s_std, 1)
            act.wait_ge(s_norm, 2)

            def norm_out(t, s):
                if not isinstance(t, int) or t >= 2:
                    act.wait_ge(s_h2d[s], half16(t, s))
                nc.scalar.activation(hn[:, s, :], x_res[:, bass.ds(t, 1), :].rearrange("p o d -> p (o d)"), ACT.Relu,
                                     bias=nmr[:, bass.ds(t, 1)], scale=rstd[:, bass.ds(t, 1)]).then_inc(s_h2, 1)
            over_tiles(act, norm_out)
            act.wait_ge(s_wgt, 1)
            indices(2)

            act.wait_ge(s_add, 3 * VISITS)

            def final_tile(t, s):
                need(act, s_fm, t + (-1))
                nc.scalar.copy(hs[:, s, :], agg[:, cols(t)]).then_inc(s_fc, 1)
            over_tiles(act, final_tile)

        @block.vector
        def _(dve):
            count = [0]

            def chain(ins):
                count[0] += 1
                ins.then_inc(s_dve, 1)
                dve.wait_ge(s_dve, count[0])

            nc.vector.memset(x_res[:, TILES - 1, :], 0.0).then_inc(s_zero, 1)
            nc.vector.memset(ones[:, :], 1.0)
            dve.wait_ge(s_iota, 3)
            nc.vector.tensor_copy(iota_f[:, :], iota_i[:, :])
            nc.vector.tensor_copy(visit_f[:, :], visit_i[:, :])
            chain(nc.vector.tensor_copy(row_f[:, :], row_i[:, :]))
            nc.vector.tensor_scalar(win_first[:, :], row_f[:, :], float(WIN), None, ALU.mult)
            chain(nc.vector.tensor_scalar(ident[:, :], iota_f[:, 0:P], row_f[:, 0:1], None, ALU.is_equal))
            nc.vector.memset(eps_c[:, :], EPS).then_inc(s_const, 1)

            dve.wait_ge(s_lastb, 16)
            chain(nc.vector.tensor_copy(last_f, last_b))
            chain(nc.vector.tensor_scalar(below_o, last_f, win_first[0:WINS, 0:1], None, ALU.is_lt, ALU.add,
                                          accum_out=start_c[0:WINS, 0:1]))
            chain(nc.vector.tensor_tensor(start_v[0:WINS, :], start_c[0:WINS, :], row_f[0:WINS, :], ALU.add))
            nc.vector.tensor_scalar(start_d[0:WINS, :], ident[0:WINS, 0:WINS], start_v[0:WINS, 0:1], None,
                                    ALU.mult).then_inc(s_diag, 1)
            dve.wait_ge(s_spread, 1)
            chain(nc.vector.tensor_copy(start_b[:, :], bank[7][:, 0:WINS]))
            with dve.Fori(0, VT) as t:
                last = nc.vector.tensor_scalar(count_o[:, 0:WINS - 1], start_b[:, 1:WINS], visit_f[:, bass.ds(t, 1)], None,
                                               ALU.is_le, ALU.add, accum_out=win_v[:, bass.ds(t, 1)])
                last.then_inc(s_dve, 1)
                dve.wait_ge(s_dve, t + (count[0] + 1))
            count[0] += VT
            chain(nc.vector.tensor_tensor(chunk_v[:, :], visit_f[:, :], win_v[:, :], ALU.subtract))
            chain(nc.vector.tensor_scalar(chunk_v[:, :], chunk_v[:, :], float(CHUNKS - 1), None, ALU.min))
            chain(nc.vector.tensor_tensor(first_v[:, :], visit_f[:, :], chunk_v[:, :], ALU.subtract))
            chain(nc.vector.tensor_scalar(first_v[:, :], first_v[:, :], float(WIN), None, ALU.mult))
            nc.vector.tensor_copy(chunk_i[:, :], chunk_v[:, :]).then_inc(s_chunks, 1)
            nc.vector.tensor_scalar(base_v[:, :], first_v[:, :], float(WIN * (WINS - 1)), None, ALU.min).then_inc(s_chunks, 1)
            dve.wait_ge(s_baseT, 1)
            nc.vector.tensor_copy(base_r[0:VT, :], bank[6][0:VT, 0:P]).then_inc(s_baser, 1)

            def convert(t, s):
                dve.wait_ge(s_raw[s], t * 40 + (80 - 40 * s))
                need(dve, s_tabT, t + (-1))
                nc.vector.tensor_scalar(conv[:, s, 0, :], raw[:, s, 0, :], first_v[:, bass.ds(t, 1)], None, ALU.subtract)
                nc.vector.scalar_tensor_tensor(conv[:, s, 1, :], raw[:, s, 1, :], float(R), raw[:, s, 2, :], ALU.mult, ALU.add)
                nc.vector.tensor_copy(conv[:, s, 2, :], raw[:, s, 3, :])
                nc.vector.tensor_copy(conv[:, s, 3, :], raw[:, s, 4, :]).then_inc(s_conv, 1)
            over_visit_tiles(dve, convert)

            dve.wait_ge(s_x, 80)

            def tile_stats(t):
                nc.vector.bn_stats(stats[:, bass.ds(t, 1), :].rearrange("p o d -> p (o d)"),
                                   x_res[:, bass.ds(t, 1), :].rearrange("p o d -> p (o d)")).then_inc(s_bn, 1)

            def norm_factors(turn):
                dve.wait_ge(s_bn, turn * TILES)
                nc.vector.tensor_tensor(mean[:, :], stats[:, :, 1], stats[:, :, 4], ALU.add)
                nc.vector.tensor_tensor(gap[:, :], stats[:, :, 1], stats[:, :, 4], ALU.subtract)
                chain(nc.vector.tensor_tensor(var[:, :], stats[:, :, 2], stats[:, :, 5], ALU.add))
                nc.vector.tensor_scalar(mean[:, :], mean[:, :], 0.5, None, ALU.mult)
                chain(nc.vector.tensor_tensor(gap[:, :], gap[:, :], gap[:, :], ALU.mult))
                chain(nc.vector.tensor_scalar(gap[:, :], gap[:, :], 0.25, None, ALU.mult))
                nc.vector.scalar_tensor_tensor(var[:, :], var[:, :], 1.0 / D, gap[:, :], ALU.mult, ALU.add).then_inc(s_var, 1)
                dve.wait_ge(s_std, turn)
                chain(nc.vector.reciprocal(rstd[:, :], std[:, :]))
                nc.vector.scalar_tensor_tensor(nmr[:, :], mean[:, :], -1.0, rstd[:, :], ALU.mult, ALU.mult).then_inc(s_norm, 1)

            with dve.Fori(0, TILES) as t:
                tile_stats(t)
            norm_factors(1)

            def stationary(t, s):
                dve.wait_ge(s_hT, t + 1)
                need(dve, s_xf, t + (-1))
                nc.vector.tensor_copy(hs[:, s, :], bank[4 + s][:, 0:P]).then_inc(s_hs, 1)

            def evac(layer):
                def step(t, s):
                    dve.wait_ge(s_xf, t + (layer * TILES + 1))
                    if layer or not isinstance(t, int) or t >= 2:
                        stored(dve, layer, t, s)
                    nc.vector.tensor_copy(xts[:, s, HT:TAB], bank[2 * s + 1][:, 0:HT]).then_inc(s_evd, 1)
                    nc.vector.tensor_scalar(agg[:, cols(t)], bank[6 + s][:, 0:P], b_col[:, 0:1], None,
                                            ALU.add).then_inc(s_ag, 1)
                return step
            dve.wait_ge(s_w, 96)
            lagged_tiles(dve, stationary, evac(0))

            nc.vector.memset(alpha_sb[:, 0:1], 0.0).then_inc(s_const, 1)
            dve.wait_ge(s_const, 2)
            dve.wait_ge(s_base, 16)
            dve.wait_ge(s_tab, VT)
            dve.wait_ge(s_ag, TILES)

            def aggregate(layer, lookup):
                def step(j, n):
                    bases = []

                    def build_onehot(k):
                        if k in [first for first, _ in GROUPS]:
                            g = [first for first, _ in GROUPS].index(k)
                            dve.wait_ge(s_place, n * NG + (g + 1))
                        if layer < 2:
                            ins = nc.vector.tensor_scalar(onehot[:, k % RING, :], iota_f[:, 0:WIN], place_s[:, k:k + 1], None,
                                                          ALU.is_equal)
                        else:
                            ins = nc.vector.tensor_scalar(onehot[:, k % RING, :], iota_f[:, 0:WIN], place_s[:, k:k + 1],
                                                          type_s[:, k:k + 1], ALU.is_equal, ALU.mult)
                        ins.then_inc(s_oh, 1)
                    for k in range(LOOKAHEAD):
                        build_onehot(k)
                    if lookup:
                        need(dve, s_alpha, n)
                    for k in range(BLOCK):
                        for first, size in GROUPS:
                            if k == first:
                                _, values = nc.values_load_multi_w_load_instructions(
                                    base_t[0:1, bass.ds(j * BLOCK + first, size)], engines=[dve.engine],
                                    min_val=0, max_val=WIN * (WINS - 1),
                                    skip_runtime_bounds_check_because="written with a minimum against the last window's first column")
                                bases.extend(values)
                        if k + LOOKAHEAD < BLOCK:
                            build_onehot(k + LOOKAHEAD)
                        need(dve, s_add, n * BLOCK + k)
                        if lookup:
                            nc.vector.scalar_tensor_tensor(look_o[:, k % RING, :], iota_f[:, 0:TYPES], type_s[:, k:k + 1],
                                                           alpha_sb[:, :], ALU.is_equal, ALU.mult,
                                                           accum_out=alpha_s[:, k:k + 1]).then_inc(s_look, 1)
                        dve.wait_ge(s_mm, n * BLOCK + (k + 1))
                        window = agg[:, bass.ds(bases[k], WIN)]
                        nc.vector.tensor_tensor(window, window, bank[k % RING][:, 0:WIN], ALU.add).then_inc(s_add, 1)
                over_blocks(dve, layer, step)

            aggregate(0, True)
            dve.wait_ge(s_w2, 48)
            over_tiles(dve, evac(1))
            dve.wait_ge(s_ag, 2 * TILES)
            aggregate(1, True)
            dve.wait_ge(s_alpha, 2 * BLOCKS)
            nc.vector.tensor_tensor(type_t[:, :], type_t[:, :], rtype_t[:, :], ALU.add)
            nc.vector.tensor_single_scalar(index_t[:, :], index_t[:, :], R.bit_length() - 1,
                                           ALU.logical_shift_right).then_inc(s_wgt, 1)

            def residual(t, s):
                tile = x_res[:, bass.ds(t, 1), :].rearrange("p o d -> p (o d)")
                dve.wait_ge(s_rT, t + 1)
                need(dve, s_rx, t)
                nc.vector.tensor_tensor(tile, tile, bank[4 + s][:, 0:P], ALU.add).then_inc(s_rx, 1)
                if not isinstance(t, int) or t > 0:
                    tile_stats(t + (-1))
            over_tiles(dve, residual)
            dve.wait_ge(s_rx, TILES)
            tile_stats(TILES - 1)
            norm_factors(2)
            nc.vector.memset(agg[:, :], 0.0).then_inc(s_dve, 1)
            count[0] += 1
            def add_bias(t, s):
                tile = x_res[:, bass.ds(t, 1), :].rearrange("p o d -> p (o d)")
                dve.wait_ge(s_h2, t + 1)
                nc.vector.tensor_tensor(tile, tile, bias_sb[:, :], ALU.add).then_inc(s_h2b, 1)
            over_tiles(dve, add_bias)
            dve.wait_ge(s_h2b, TILES)
            dve.wait_ge(s_dve, count[0])
            dve.wait_ge(s_wgt, 1)
            aggregate(2, False)

            def final(t, s):
                tile = x_res[:, bass.ds(t, 1), :].rearrange("p o d -> p (o d)")
                dve.wait_ge(s_fm, t + 1)
                nc.vector.tensor_tensor(tile, tile, bank[4 + s][:, 0:P], ALU.add).then_inc(s_fa, 1)
            over_tiles(dve, final)

        @block.tensor
        def _(pe):
            pe.wait_ge(s_diag, 1)
            nc.tensor.matmul(bank[7][:, 0:WINS], ones[0:WINS, :], start_d[0:WINS, :], start=True, stop=True).then_inc(s_spread, 1)
            pe.wait_ge(s_chunks, 2)
            nc.tensor.transpose(bank[6][0:VT, 0:P], base_v[:, :], ident[:, :]).then_inc(s_baseT, 1)

            def table_tile(t, s):
                pe.wait_ge(s_conv, t + 1)
                need(pe, s_tab, t + (-1))
                for a in range(4):
                    last = nc.tensor.transpose(bank[s][:, a * P:(a + 1) * P], conv[:, s, a, :], ident[:, :])
                last.then_inc(s_tabT, 1)
            over_visit_tiles(pe, table_tile)
            pe.wait_ge(s_tab, VT)
            pe.wait_ge(s_baser, 1)

            def transpose_tile(t, s):
                pe.wait_ge(s_hn, t + 1)
                need(pe, s_hs, t + (-1))
                nc.tensor.transpose(bank[4 + s][:, 0:P], hn[:, s, :], ident[:, :]).then_inc(s_hT, 1)

            def transform(layer):
                def step(t, s):
                    pe.wait_ge(s_hs, t + (layer * TILES + 1))
                    need(pe, s_eva, t + (layer * TILES - 1))
                    need(pe, s_ag, t + (layer * TILES - 1))
                    for half in range(2):
                        nc.tensor.matmul(bank[2 * s + half][:, 0:HT], hs[:, s, :],
                                         w_sb[:, half * R // 2:(half + 1) * R // 2, :].rearrange("p r d -> p (r d)"),
                                         start=True, stop=True)
                    nc.tensor.matmul(bank[6 + s][:, 0:P], sl_sb[:, :], hs[:, s, :], start=True, stop=True).then_inc(s_xf, 1)
                return step
            pe.wait_ge(s_w, 96)
            lagged_tiles(pe, transpose_tile, transform(0))

            def products(layer):
                def step(j, n):
                    for g, (first, size) in enumerate(GROUPS):
                        pe.wait_ge(s_g[g], n * (16 * size) + 16 * size)
                        for k in range(first, first + size):
                            need(pe, s_add, n * BLOCK + (k - LOOKAHEAD))
                            pe.wait_ge(s_oh, n * BLOCK + (k + 1))
                            nc.tensor.matmul(bank[k % RING][:, 0:WIN], msgs[:, k, :], onehot[:, k % RING, :],
                                             start=True, stop=True).then_inc(s_mm, 1)
                over_blocks(pe, layer, step)
            pe.wait_ge(s_eva, TILES)
            pe.wait_ge(s_ag, TILES)
            products(0)
            pe.wait_ge(s_w2, 48)
            pe.wait_ge(s_add, VISITS)
            over_tiles(pe, transform(1))
            pe.wait_ge(s_eva, 2 * TILES)
            pe.wait_ge(s_ag, 2 * TILES)
            products(1)

            def transpose_relu(t, s):
                pe.wait_ge(s_rl, t + 1)
                need(pe, s_rx, t + (-1))
                nc.tensor.transpose(bank[4 + s][:, 0:P], hs[:, s, :], ident[:, :]).then_inc(s_rT, 1)
            over_tiles(pe, transpose_relu)
            pe.wait_ge(s_rx, TILES)
            products(2)

            def final_product(t, s):
                pe.wait_ge(s_fc, t + 1)
                need(pe, s_fa, t + (-1))
                nc.tensor.matmul(bank[4 + s][:, 0:P], hs[:, s, :], weight_sb[:, :], start=True, stop=True).then_inc(s_fm, 1)
            over_tiles(pe, final_product)


_INS = ["x", "src", "dst", "edge_type_201", "edge_type_8", "L0_gnn_w1", "L0_gnn_sl1", "L0_gnn_b1", "L0_gnn_w2",
        "L0_gnn_sl2", "L0_gnn_b2", "L1_gnn_weight", "L1_gnn_alpha", "L1_gnn_bias"]


def kernel(**inputs):
    import numpy as _np
    import concourse.bacc as _bacc
    from concourse import mybir as _mybir
    from concourse.bass_utils import run_bass_kernel_spmd as _run

    nc = _bacc.Bacc("TRN2", target_bir_lowering=False, num_devices=1)
    arrays, args = {}, []
    for name in _INS:
        a = _np.ascontiguousarray(inputs[name])
        arrays[f"in_{name}_dram"] = a
        args.append(nc.dram_tensor(f"in_{name}_dram", a.shape, _mybir.dt.from_np(a.dtype), kind="ExternalInput").ap())
    args.append(nc.dram_tensor("out_0_dram", inputs["x"].shape, _mybir.dt.float32, kind="ExternalOutput").ap())
    build(nc, *args)
    r = _run(nc, [arrays], core_ids=[0])
    return r.results[0]["out_0_dram"]
```

```python
from contextlib import ExitStack

import concourse.bass as bass
from concourse import mybir

P = 128
WIN = 256
BLOCK = 19
LOOKAHEAD = 2
RING = 4
EPS = 1e-5
FAR = 1 << 20


def split(n, most=8192):
    for unit in (16, 10, 5, 2, 1):
        for rows in range(unit, n + 1, unit):
            if n % rows == 0 and n // rows <= most:
                return rows, n // rows


def build(nc, x, src, dst, etype, rel, w1, sl1, b1, w2, sl2, b2, weight, alpha, bias, out):
    fp32, i32, i16 = mybir.dt.float32, mybir.dt.int32, mybir.dt.int16
    ALU = mybir.AluOpType
    ACT = mybir.ActivationFunctionType

    NODES, D = x.shape
    EDGES = src.shape[0]
    R = w1.shape[0]
    TYPES = alpha.shape[0]
    TILES = -(-NODES // P)
    TAIL = NODES - (TILES - 1) * P
    CHUNKS = EDGES // P
    WINS = -(-NODES // WIN)
    VISITS = -(-(CHUNKS + WINS - 1) // BLOCK) * BLOCK
    BLOCKS = VISITS // BLOCK
    VT = -(-VISITS // P)
    HALF = (EDGES - NODES) // 2
    COLS = TILES * P
    assert TILES % 2 == 0 and TILES >= 4 and D == P and EDGES % P == 0 and VT >= 3 and WINS * WIN >= NODES
    GROUPS = [(g, min(5, BLOCK - g)) for g in range(0, BLOCK, 5)]
    NG = len(GROUPS)
    LR = max(r for r in range(1, P + 1) if CHUNKS % r == 0)
    LC = CHUNKS // LR
    TAB = R * D
    HT = TAB // 2

    xt1 = nc.dram_tensor("xt1", (COLS * R, D), fp32, kind="Internal").ap()
    xt2 = nc.dram_tensor("xt2", (COLS * R, D), fp32, kind="Internal").ap()
    h2_d = nc.dram_tensor("h2_d", (COLS, D), fp32, kind="Internal").ap()
    row_d = nc.dram_tensor("row_d", (EDGES,), i32, kind="Internal").ap()
    tet_d = nc.dram_tensor("tet_d", (EDGES,), i32, kind="Internal").ap()
    last_d = nc.dram_tensor("last_d", (CHUNKS,), i32, kind="Internal").ap()
    base_d = nc.dram_tensor("base_d", (VT * P,), i32, kind="Internal").ap()

    with ExitStack() as ctx:
        def sb(name, shape, dt=fp32):
            return ctx.enter_context(nc.sbuf_tensor(name, shape, dt))

        def sem(name):
            return ctx.enter_context(nc.semaphore(name))

        x_res = sb("x_res", [P, TILES, D])
        agg = sb("agg", [P, COLS])
        tables = sb("tables", [P, 4, VT * P])
        place_t, index_t, type_t, rtype_t = (tables[:, a, :] for a in range(4))
        base_t = sb("base_t", [1, VT * P], i32)
        iota_i = sb("iota_i", [P, max(WIN, TYPES)], i32)
        iota_f = sb("iota_f", [P, max(WIN, TYPES)])
        row_i = sb("row_i", [P, 1], i32)
        row_f = sb("row_f", [P, 1])
        visit_i = sb("visit_i", [P, VT], i32)
        visit_f = sb("visit_f", [P, VT])
        win_first = sb("win_first", [P, 1])
        ident = sb("ident", [P, P])
        ones = sb("ones", [P, P])
        eps_c = sb("eps_c", [P, 1])
        w_sb = sb("w_sb", [P, R, D])
        sl_sb = sb("sl_sb", [P, D])
        b_col = sb("b_col", [P, 1])
        weight_sb = sb("weight_sb", [P, D])
        bias_sb = sb("bias_sb", [P, D])
        alpha_sb = sb("alpha_sb", [P, TYPES])
        last_sb = sb("last_sb", [P, LC], i32)
        start_c = sb("start_c", [P, 1])
        start_v = sb("start_v", [P, 1])
        start_d = sb("start_d", [P, WINS])
        start_b = sb("start_b", [P, WINS])
        count_o = sb("count_o", [P, WINS])
        win_v = sb("win_v", [P, VT])
        chunk_v = sb("chunk_v", [P, VT])
        chunk_i = sb("chunk_i", [P, VT], i32)
        first_v = sb("first_v", [P, VT])
        base_v = sb("base_v", [P, VT])
        base_r = sb("base_r", [P, P], i32)
        descent_c = sb("descent_c", [P, 1])
        unsorted = sb("unsorted", [P, 1])
        unsorted_far = sb("unsorted_far", [P, 1])
        unsorted_i = sb("unsorted_i", [P, 1], i32)
        step_v = sb("step_v", [P, 1])
        place_g = sb("place_g", [P, 1])
        stats = sb("stats", [P, TILES, 6])
        mean = sb("mean", [P, TILES])
        gap = sb("gap", [P, TILES])
        var = sb("var", [P, TILES])
        std = sb("std", [P, TILES])
        rstd = sb("rstd", [P, TILES])
        nmr = sb("nmr", [P, TILES])
        hn = sb("hn", [P, 2, P])
        hs = sb("hs", [P, 2, P])
        xts = sb("xts", [P, 2, TAB])
        index_s = sb("index_s", [P, BLOCK], i32)
        msgs = sb("msgs", [P, BLOCK, D])
        conv = msgs[:, 0:8, :].rearrange("p (s a) e -> p s a e", s=2)
        onehot = sb("onehot", [P, RING, WIN])
        place_s = sb("place_s", [P, BLOCK])
        type_s = sb("type_s", [P, BLOCK])
        alpha_s = sb("alpha_s", [P, BLOCK])
        look_o = sb("look_o", [P, RING, TYPES])
        bank = [ctx.enter_context(nc.psum_tensor(f"bank{i}", [P, 512], fp32)) for i in range(8)]

        last_b = index_t[0:WINS, 0:CHUNKS].bitcast(i32)
        last_f = place_t[0:WINS, 0:CHUNKS]
        below_o = type_t[0:WINS, 0:CHUNKS]

        here = agg[:, 0:CHUNKS].bitcast(i32)
        after = agg[:, CHUNKS:2 * CHUNKS].bitcast(i32)
        descends = agg[:, 0:CHUNKS]
        source_e = agg[:, 2 * CHUNKS:3 * CHUNKS].bitcast(i32)
        rel_e = rtype_t[:, 0:CHUNKS].bitcast(i32)
        assert 3 * CHUNKS <= COLS and EDGES == P * CHUNKS

        s_end = sem("end_of_destinations_set")
        s_pairs = sem("destination_pairs_loaded")
        s_x = sem("x_loaded")
        s_dst = sem("last_loaded")
        s_last = sem("last_stored")
        s_lastb = sem("last_broadcast")
        s_tet = sem("reverse_types_stored")
        s_w = sem("weights_loaded")
        s_w2 = sem("second_weights_loaded")
        s_zero = sem("tail_tile_cleared")
        s_iota = sem("iotas_written")
        s_const = sem("constants_written")
        s_dve = sem("vector_step_done")
        s_desc = sem("descents_counted")
        s_desum = sem("descents_summed")
        s_flag = sem("order_flag_ready")
        s_diag = sem("window_starts_on_diagonal")
        s_spread = sem("window_starts_broadcast")
        s_chunks = sem("visit_chunks_written")
        s_baseT = sem("bases_transposed")
        s_baser = sem("base_rows_written")
        s_based = sem("bases_stored")
        s_base = sem("bases_loaded")
        s_edges = sem("sources_and_relations_loaded")
        s_row = sem("edge_rows_computed")
        s_rowd = sem("edge_rows_stored")
        s_raw = sem("table_rows_gathered")
        s_conva = sem("rows_and_types_converted")
        s_convd = sem("places_converted")
        s_tabT = sem("table_transposed")
        s_taba = sem("places_and_rows_in_table")
        s_tabd = sem("types_in_table")
        s_bn = sem("tile_stats_done")
        s_var = sem("variances_ready")
        s_std = sem("std_ready")
        s_norm = sem("norm_factors_ready")
        s_hn = sem("normed_tile_ready")
        s_hT = sem("normed_tile_transposed")
        s_hs = sem("stationary_tile_ready")
        s_xf = sem("tile_transformed")
        s_eva = sem("left_half_evacuated")
        s_evd = sem("right_half_evacuated")
        s_ag = sem("self_term_in_agg")
        s_xts = [sem("tile_rows_stored_0"), sem("tile_rows_stored_1")]
        s_idx = sem("index_group_ready")
        s_g = [sem(f"group_gathered_{g}") for g in range(NG)]
        s_oh = sem("onehot_ready")
        s_mm = sem("product_done")
        s_add = sem("product_added")
        s_place = sem("places_and_types_ready")
        s_look = sem("alpha_looked_up")
        s_alpha = sem("alphas_kept")
        g_open = sem("general_block_open")
        g_place = sem("general_place_ready")
        g_oh = sem("general_onehot_ready")
        g_mm = sem("general_product_done")
        s_wgt = sem("edge_weights_ready")
        s_rl = sem("relu_tile_ready")
        s_rT = sem("relu_tile_transposed")
        s_rx = sem("residual_added")
        s_h2 = sem("second_norm_tile_ready")
        s_h2b = sem("bias_added")
        s_h2d = [sem("second_norm_stored_0"), sem("second_norm_stored_1")]
        s_fc = sem("final_stationary_ready")
        s_fm = sem("final_product_done")
        s_fa = sem("final_added")
        s_out = sem("output_stored")

        block = ctx.enter_context(nc.Block())

        def need(eng, s, value):
            if not isinstance(value, int) or value > 0:
                eng.wait_ge(s, value)

        def over_tiles(eng, step):
            step(0, 0)
            step(1, 1)
            with eng.Fori(1, TILES // 2) as i:
                step(i * 2, 0)
                step(i * 2 + 1, 1)

        def lagged(eng, tiles, ahead, behind):
            ahead(0, 0)
            ahead(1, 1)
            behind(0, 0)
            ahead(2, 0)
            behind(1, 1)
            turns = (tiles - 3) // 2
            if turns:
                with eng.Fori(1, turns + 1) as i:
                    ahead(i * 2 + 1, 1)
                    behind(i * 2, 0)
                    ahead(i * 2 + 2, 0)
                    behind(i * 2 + 1, 1)
            for t in range(2 * turns + 2, tiles):
                if t + 1 < tiles:
                    ahead(t + 1, (t + 1) % 2)
                behind(t, t % 2)

        def over_blocks(eng, layer, step):
            step(0, layer * BLOCKS)
            with eng.Fori(1, BLOCKS) as j:
                step(j, j + layer * BLOCKS)

        def cols(t, width=P):
            return bass.ds(t * width, width)

        def half16(t, s):
            return t * 8 + (-8 * s)

        def stored(eng, layer, t, s):
            eng.wait_ge(s_xts[s], t * 8 + (8 * layer * TILES - 8 * s))

        @block.sync
        def _(sp):
            with nc.allow_non_contiguous_dma("last destination of each chunk, biases as columns"):
                sp.dma_start(last_sb[0:LR, 0:LC],
                             dst.rearrange("(a b p) -> a b p", a=LR, p=P)[:, :, P - 1]).then_inc(s_dst, 16)
            cuts = [(TILES - 1) * q // 4 for q in range(5)]
            for a, b in zip(cuts, cuts[1:]):
                sp.dma_start(x_res[:, a:b, :], x[a * P:b * P, :].rearrange("(t p) d -> p t d", p=P)).then_inc(s_x, 16)
            sp.wait_ge(s_zero, 1)
            sp.dma_start(x_res[0:TAIL, TILES - 1, :], x[(TILES - 1) * P:NODES, :]).then_inc(s_x, 16)
            sp.dma_start(source_e, src.rearrange("(p c) -> p c", p=P)).then_inc(s_edges, 16)
            sp.dma_start(rel_e, rel.rearrange("(p c) -> p c", p=P)).then_inc(s_edges, 16)
            sp.dma_start(here, dst.rearrange("(p c) -> p c", p=P)).then_inc(s_pairs, 16)
            sp.wait_ge(s_end, 1)
            sp.dma_start(after[0:P - 1, :], dst[1:1 + (P - 1) * CHUNKS].rearrange("(p c) -> p c", c=CHUNKS)).then_inc(s_pairs, 16)
            sp.dma_start(after[P - 1:P, 0:CHUNKS - 1],
                         dst[1 + (P - 1) * CHUNKS:EDGES].rearrange("(o c) -> o c", o=1)).then_inc(s_pairs, 16)
            sp.wait_ge(s_dst, 16)
            sp.dma_start(last_d.rearrange("(a b) -> a b", a=LR), last_sb[0:LR, 0:LC]).then_inc(s_last, 16)
            for to, frm, n in ((0, HALF, HALF), (HALF, 0, HALF), (2 * HALF, 2 * HALF, NODES)):
                a, _b = split(n)
                sp.dma_start(tet_d[to:to + n].rearrange("(a b) -> a b", a=a),
                             etype[frm:frm + n].rearrange("(a b) -> a b", a=a)).then_inc(s_tet, 16)
            sp.wait_ge(s_last, 16)
            sp.dma_start(last_b, last_d.partition_broadcast(WINS)).then_inc(s_lastb, 16)
            sp.dma_start(w_sb[:, :, :], w1.rearrange("r d e -> d r e")).then_inc(s_w, 16)
            sp.dma_start(sl_sb[:, :], sl1).then_inc(s_w, 16)
            sp.dma_start(weight_sb[:, :], weight).then_inc(s_w, 16)
            with nc.allow_non_contiguous_dma("biases as columns"):
                sp.dma_start(b_col[:, :], b1.rearrange("(d o) -> d o", o=1)).then_inc(s_w, 16)
                sp.dma_start(bias_sb[:, :], bias.partition_broadcast(P)).then_inc(s_w, 16)
                sp.dma_start(alpha_sb[:, :], alpha.rearrange("r o -> (r o)").partition_broadcast(P)).then_inc(s_w, 16)
            sp.wait_ge(s_row, 1)
            sp.dma_start(row_d.rearrange("(p c) -> p c", p=P), source_e).then_inc(s_rowd, 16)
            sp.wait_ge(s_baser, 1)
            sp.dma_start(base_d.rearrange("(t p) -> t p", p=P), base_r[0:VT, :]).then_inc(s_based, 16)
            sp.wait_ge(s_based, 16)
            sp.dma_start(base_t[:, :], base_d.rearrange("(o n) -> o n", o=1)).then_inc(s_base, 16)

            def store_rows(layer, table):
                def step(t, s):
                    done = t + (layer * TILES + 1)
                    need(sp, s_eva, done)
                    need(sp, s_evd, done)
                    rows = table.rearrange("(n r) d -> n (r d)", r=R)
                    sp.dma_start(rows[cols(t), :], xts[:, s, :]).then_inc(s_xts[s], 16)
                over_tiles(sp, step)

            store_rows(0, xt1)
            sp.wait_ge(s_xf, TILES)
            sp.wait_ge(s_ag, TILES)
            sp.dma_start(w_sb[:, :, :], w2.rearrange("r d e -> d r e")).then_inc(s_w2, 16)
            sp.dma_start(sl_sb[:, :], sl2).then_inc(s_w2, 16)
            with nc.allow_non_contiguous_dma("biases as columns"):
                sp.dma_start(b_col[:, :], b2.rearrange("(d o) -> d o", o=1)).then_inc(s_w2, 16)
            store_rows(1, xt2)

            def store_h2(t, s):
                sp.wait_ge(s_h2, t + 1)
                sp.dma_start(h2_d[cols(t), :], hn[:, s, :]).then_inc(s_h2d[s], 16)
            over_tiles(sp, store_h2)

            for a, b in zip(cuts, cuts[1:]):
                sp.wait_ge(s_fa, b)
                sp.dma_start(out[a * P:b * P, :].rearrange("(t p) d -> p t d", p=P), x_res[:, a:b, :]).then_inc(s_out, 16)
            sp.wait_ge(s_fa, TILES)
            sp.dma_start(out[(TILES - 1) * P:NODES, :], x_res[0:TAIL, TILES - 1, :]).then_inc(s_out, 16)
            sp.wait_ge(s_out, 80)

        @block.gpsimd
        def _(pool):
            nc.gpsimd.iota(iota_i[:, :], pattern=[[1, max(WIN, TYPES)]], base=0, channel_multiplier=0).then_inc(s_iota, 1)
            nc.gpsimd.iota(row_i[:, :], pattern=[[0, 1]], base=0, channel_multiplier=1).then_inc(s_iota, 1)
            nc.gpsimd.iota(visit_i[:, :], pattern=[[P, VT]], base=0, channel_multiplier=1).then_inc(s_iota, 1)

            arrays = [a.rearrange("(c p) -> c p", p=P) for a in (dst, row_d, etype, tet_d)]
            pool.wait_ge(s_tet, 48)
            pool.wait_ge(s_rowd, 16)

            pool.wait_ge(s_chunks, 1)
            for t in range(VT):
                for a in range(4):
                    pool.indirect_dma_start(out=tables[:, a, t * P:(t + 1) * P].bitcast(i32), out_offset=None, in_=arrays[a],
                                            in_offset=bass.IndirectOffsetOnAxis(ap=chunk_i[:, t:t + 1], axis=0)
                                            ).then_inc(s_raw, 16)

            def gather_layer(layer, table):
                def step(j, n):
                    for g, (first, size) in enumerate(GROUPS):
                        pool.wait_ge(s_idx, n * NG + (g + 1))
                        need(pool, s_mm, n * BLOCK + (first + size - BLOCK))
                        pool.nop(nofuse=True)
                        for k in range(first, first + size):
                            pool.indirect_dma_start(out=msgs[:, k, :], out_offset=None, in_=table,
                                                    in_offset=bass.IndirectOffsetOnAxis(ap=index_s[:, k:k + 1], axis=0)
                                                    ).then_inc(s_g[g], 16)
                over_blocks(pool, layer, step)

            for layer, table in ((0, xt1), (1, xt2)):
                for s in range(2):
                    pool.wait_ge(s_xts[s], 16 * (layer + 1) * (TILES // 2))
                gather_layer(layer, table)
            for s in range(2):
                pool.wait_ge(s_h2d[s], 16 * (TILES // 2))
            gather_layer(2, h2_d)

        @block.scalar
        def _(act):
            act.wait_ge(s_var, 1)
            act.wait_ge(s_const, 1)
            nc.scalar.activation(std[:, :], var[:, :], ACT.Sqrt, bias=eps_c[:, 0:1]).then_inc(s_std, 1)
            act.wait_ge(s_norm, 1)

            def norm_tile(t, s):
                need(act, s_hT, t + (-1))
                nc.scalar.activation(hn[:, s, :], x_res[:, bass.ds(t, 1), :].rearrange("p o d -> p (o d)"), ACT.Relu,
                                     bias=nmr[:, bass.ds(t, 1)], scale=rstd[:, bass.ds(t, 1)]).then_inc(s_hn, 1)

            def relu_tile(t, s):
                need(act, s_xf, t + (TILES - 1))
                nc.scalar.activation(hs[:, s, :], agg[:, cols(t)], ACT.Relu).then_inc(s_hs, 1)

            def evac(layer):
                def step(t, s):
                    act.wait_ge(s_xf, t + (layer * TILES + 1))
                    if layer or not isinstance(t, int) or t >= 2:
                        stored(act, layer, t, s)
                    nc.scalar.copy(xts[:, s, 0:HT], bank[2 * s][:, 0:HT]).then_inc(s_eva, 1)
                return step

            evac_first = evac(0)
            norm_tile(0, 0)
            norm_tile(1, 1)
            for t in range(2):
                norm_tile(t + 2, t % 2)
                evac_first(t, t % 2)
            with act.Fori(1, TILES // 2 - 1) as i:
                norm_tile(i * 2 + 2, 0)
                evac_first(i * 2, 0)
                norm_tile(i * 2 + 3, 1)
                evac_first(i * 2 + 1, 1)
            evac_first(TILES - 2, 0)
            evac_first(TILES - 1, 1)

            act.wait_ge(s_raw, VT * 64)

            def convert_rest(t, s):
                need(act, s_tabT, t + (-1))
                nc.scalar.copy(conv[:, s, 1:4, :], tables[:, 1:4, cols(t)].bitcast(i32)).then_inc(s_conva, 1)

            def left_tables(t, s):
                act.wait_ge(s_tabT, t + 1)
                act.wait_ge(s_convd, t + 1)
                nc.scalar.copy(tables[:, 0:2, cols(t)],
                               bank[s][:, 0:2 * P].rearrange("p (a e) -> p a e", a=2)).then_inc(s_taba, 1)
            lagged(act, VT, convert_rest, left_tables)

            def indices(layer, types=None):
                def keep(j, n):
                    act.wait_ge(s_look, n * BLOCK + BLOCK)
                    nc.scalar.copy(types[:, bass.ds(j * BLOCK, BLOCK)], alpha_s[:, :]).then_inc(s_alpha, 1)

                def step(j, n):
                    for g, (first, size) in enumerate(GROUPS):
                        slots = slice(first, first + size)
                        columns = bass.ds(j * BLOCK + first, size)
                        need(act, s_g[g], n * (16 * size))
                        nc.scalar.copy(index_s[:, slots], (index_t if layer < 2 else index_t.bitcast(i32))[:, columns]
                                       ).then_inc(s_idx, 1)
                        need(act, s_add, n * BLOCK + (first + size - BLOCK))
                        nc.scalar.copy(place_s[:, slots], place_t[:, columns])
                        nc.scalar.copy(type_s[:, slots], (type_t if types is None else types)[:, columns]).then_inc(s_place, 1)
                        if g == NG - 1 and types is not None and not (isinstance(j, int) and j == 0):
                            keep(j + (-1), n + (-1))
                over_blocks(act, layer, step)
                if types is not None:
                    keep(BLOCKS - 1, (layer + 1) * BLOCKS - 1)

            act.wait_ge(s_tabd, VT)
            indices(0, type_t)
            act.wait_ge(s_add, VISITS)
            lagged(act, TILES, relu_tile, evac(1))
            indices(1, rtype_t)

            act.wait_ge(s_add, 2 * VISITS)

            def relu_out(t, s):
                need(act, s_rT, t + (-1))
                nc.scalar.activation(hs[:, s, :], agg[:, cols(t)], ACT.Relu).then_inc(s_rl, 1)
            over_tiles(act, relu_out)

            act.wait_ge(s_var, 2)
            nc.scalar.activation(std[:, :], var[:, :], ACT.Sqrt, bias=eps_c[:, 0:1]).then_inc(s_std, 1)
            act.wait_ge(s_norm, 2)

            def norm_out(t, s):
                if not isinstance(t, int) or t >= 2:
                    act.wait_ge(s_h2d[s], half16(t, s))
                nc.scalar.activation(hn[:, s, :], x_res[:, bass.ds(t, 1), :].rearrange("p o d -> p (o d)"), ACT.Relu,
                                     bias=nmr[:, bass.ds(t, 1)], scale=rstd[:, bass.ds(t, 1)]).then_inc(s_h2, 1)
            over_tiles(act, norm_out)
            act.wait_ge(s_wgt, 1)
            indices(2)

            act.wait_ge(s_add, 3 * VISITS)

            def final_tile(t, s):
                need(act, s_fm, t + (-1))
                nc.scalar.copy(hs[:, s, :], agg[:, cols(t)]).then_inc(s_fc, 1)
            over_tiles(act, final_tile)

        @block.vector
        def _(dve):
            count = [0]

            def chain(ins):
                count[0] += 1
                ins.then_inc(s_dve, 1)
                dve.wait_ge(s_dve, count[0])

            nc.vector.memset(x_res[:, TILES - 1, :], 0.0).then_inc(s_zero, 1)
            nc.vector.memset(after[:, CHUNKS - 1:CHUNKS], FAR).then_inc(s_end, 1)
            nc.vector.memset(ones[:, :], 1.0)
            dve.wait_ge(s_iota, 3)
            nc.vector.tensor_copy(iota_f[:, :], iota_i[:, :])
            nc.vector.tensor_copy(visit_f[:, :], visit_i[:, :])
            chain(nc.vector.tensor_copy(row_f[:, :], row_i[:, :]))
            nc.vector.tensor_scalar(win_first[:, :], row_f[:, :], float(WIN), None, ALU.mult)
            chain(nc.vector.tensor_scalar(ident[:, :], iota_f[:, 0:P], row_f[:, 0:1], None, ALU.is_equal))
            nc.vector.memset(eps_c[:, :], EPS).then_inc(s_const, 1)

            dve.wait_ge(s_x, 80)

            def tile_stats(t):
                nc.vector.bn_stats(stats[:, bass.ds(t, 1), :].rearrange("p o d -> p (o d)"),
                                   x_res[:, bass.ds(t, 1), :].rearrange("p o d -> p (o d)")).then_inc(s_bn, 1)

            def norm_factors(turn):
                dve.wait_ge(s_bn, turn * TILES)
                nc.vector.tensor_tensor(mean[:, :], stats[:, :, 1], stats[:, :, 4], ALU.add)
                nc.vector.tensor_tensor(gap[:, :], stats[:, :, 1], stats[:, :, 4], ALU.subtract)
                chain(nc.vector.tensor_tensor(var[:, :], stats[:, :, 2], stats[:, :, 5], ALU.add))
                nc.vector.tensor_scalar(mean[:, :], mean[:, :], 0.5, None, ALU.mult)
                chain(nc.vector.tensor_tensor(gap[:, :], gap[:, :], gap[:, :], ALU.mult))
                chain(nc.vector.tensor_scalar(gap[:, :], gap[:, :], 0.25, None, ALU.mult))
                nc.vector.scalar_tensor_tensor(var[:, :], var[:, :], 1.0 / D, gap[:, :], ALU.mult, ALU.add).then_inc(s_var, 1)
                dve.wait_ge(s_std, turn)
                chain(nc.vector.reciprocal(rstd[:, :], std[:, :]))
                nc.vector.scalar_tensor_tensor(nmr[:, :], mean[:, :], -1.0, rstd[:, :], ALU.mult, ALU.mult).then_inc(s_norm, 1)

            with dve.Fori(0, TILES) as t:
                tile_stats(t)
            norm_factors(1)

            dve.wait_ge(s_edges, 32)
            nc.vector.scalar_tensor_tensor(source_e, source_e, float(R), rel_e, ALU.mult, ALU.add).then_inc(s_row, 1)

            dve.wait_ge(s_pairs, 48)
            chain(nc.vector.tensor_tensor(descends, after, here, ALU.is_lt))
            nc.vector.reduce_sum(descent_c[:, :], descends, mybir.AxisListType.X).then_inc(s_desc, 1)
            dve.wait_ge(s_desum, 1)
            chain(nc.vector.tensor_scalar(unsorted[:, :], bank[5][:, 0:1], 1.0, None, ALU.min))
            chain(nc.vector.tensor_scalar(unsorted_far[:, :], unsorted[:, :], float(FAR), None, ALU.mult))
            nc.vector.tensor_scalar(step_v[:, :], unsorted_far[:, :], float(WIN), None, ALU.add)
            nc.vector.tensor_copy(unsorted_i[:, :], unsorted[:, :]).then_inc(s_flag, 1)

            dve.wait_ge(s_lastb, 16)
            chain(nc.vector.tensor_copy(last_f, last_b))
            chain(nc.vector.tensor_scalar(below_o, last_f, win_first[0:WINS, 0:1], None, ALU.is_lt, ALU.add,
                                          accum_out=start_c[0:WINS, 0:1]))
            chain(nc.vector.tensor_tensor(start_v[0:WINS, :], start_c[0:WINS, :], row_f[0:WINS, :], ALU.add))
            chain(nc.vector.tensor_tensor(start_v[0:WINS, :], start_v[0:WINS, :], unsorted_far[0:WINS, :], ALU.add))
            nc.vector.tensor_scalar(start_d[0:WINS, :], ident[0:WINS, 0:WINS], start_v[0:WINS, 0:1], None,
                                    ALU.mult).then_inc(s_diag, 1)
            dve.wait_ge(s_spread, 1)
            chain(nc.vector.tensor_copy(start_b[:, :], bank[7][:, 0:WINS]))
            with dve.Fori(0, VT) as t:
                last = nc.vector.tensor_scalar(count_o[:, 0:WINS - 1], start_b[:, 1:WINS], visit_f[:, bass.ds(t, 1)], None,
                                               ALU.is_le, ALU.add, accum_out=win_v[:, bass.ds(t, 1)])
                last.then_inc(s_dve, 1)
                dve.wait_ge(s_dve, t + (count[0] + 1))
            count[0] += VT
            chain(nc.vector.tensor_tensor(chunk_v[:, :], visit_f[:, :], win_v[:, :], ALU.subtract))
            chain(nc.vector.tensor_scalar(chunk_v[:, :], chunk_v[:, :], float(CHUNKS - 1), None, ALU.min))
            chain(nc.vector.tensor_tensor(first_v[:, :], visit_f[:, :], chunk_v[:, :], ALU.subtract))
            chain(nc.vector.tensor_scalar(first_v[:, :], first_v[:, :], step_v[:, 0:1], None, ALU.mult))
            nc.vector.tensor_copy(chunk_i[:, :], chunk_v[:, :]).then_inc(s_chunks, 1)
            nc.vector.tensor_scalar(base_v[:, :], first_v[:, :], float(WIN * (WINS - 1)), None, ALU.min).then_inc(s_chunks, 1)
            dve.wait_ge(s_baseT, 1)
            nc.vector.tensor_copy(base_r[0:VT, :], bank[6][0:VT, 0:P]).then_inc(s_baser, 1)

            def stationary(t, s):
                dve.wait_ge(s_hT, t + 1)
                need(dve, s_xf, t + (-1))
                nc.vector.tensor_copy(hs[:, s, :], bank[4 + s][:, 0:P]).then_inc(s_hs, 1)

            def evac(layer):
                def step(t, s):
                    dve.wait_ge(s_xf, t + (layer * TILES + 1))
                    if layer or not isinstance(t, int) or t >= 2:
                        stored(dve, layer, t, s)
                    nc.vector.tensor_copy(xts[:, s, HT:TAB], bank[2 * s + 1][:, 0:HT]).then_inc(s_evd, 1)
                    nc.vector.tensor_scalar(agg[:, cols(t)], bank[6 + s][:, 0:P], b_col[:, 0:1], None,
                                            ALU.add).then_inc(s_ag, 1)
                return step
            dve.wait_ge(s_w, 96)
            dve.wait_ge(s_rowd, 16)
            lagged(dve, TILES, stationary, evac(0))

            dve.wait_ge(s_raw, VT * 64)

            def convert_places(t, s):
                need(dve, s_tabT, t + (-1))
                nc.vector.tensor_scalar(conv[:, s, 0, :], place_t[:, cols(t)].bitcast(i32), first_v[:, bass.ds(t, 1)], None,
                                        ALU.subtract).then_inc(s_convd, 1)

            def right_tables(t, s):
                dve.wait_ge(s_tabT, t + 1)
                nc.vector.tensor_copy(tables[:, 2:4, cols(t)],
                                      bank[2 + s][:, 0:2 * P].rearrange("p (a e) -> p a e", a=2)).then_inc(s_tabd, 1)
            lagged(dve, VT, convert_places, right_tables)

            nc.vector.memset(alpha_sb[:, 0:1], 0.0).then_inc(s_const, 1)
            dve.wait_ge(s_const, 2)
            dve.wait_ge(s_base, 16)
            dve.wait_ge(s_taba, VT)
            dve.wait_ge(s_ag, TILES)

            def aggregate(layer, lookup):
                def step(j, n):
                    bases = []

                    def build_onehot(k):
                        if k in [first for first, _ in GROUPS]:
                            g = [first for first, _ in GROUPS].index(k)
                            dve.wait_ge(s_place, n * NG + (g + 1))
                        if layer < 2:
                            ins = nc.vector.tensor_scalar(onehot[:, k % RING, :], iota_f[:, 0:WIN], place_s[:, k:k + 1], None,
                                                          ALU.is_equal)
                        else:
                            ins = nc.vector.tensor_scalar(onehot[:, k % RING, :], iota_f[:, 0:WIN], place_s[:, k:k + 1],
                                                          type_s[:, k:k + 1], ALU.is_equal, ALU.mult)
                        ins.then_inc(s_oh, 1)
                    for k in range(LOOKAHEAD):
                        build_onehot(k)
                    if lookup:
                        need(dve, s_alpha, n)
                    for k in range(BLOCK):
                        for first, size in GROUPS:
                            if k == first:
                                _, values = nc.values_load_multi_w_load_instructions(
                                    base_t[0:1, bass.ds(j * BLOCK + first, size)], engines=[dve.engine],
                                    min_val=0, max_val=WIN * (WINS - 1),
                                    skip_runtime_bounds_check_because="written with a minimum against the last window's first column")
                                bases.extend(values)
                        if k + LOOKAHEAD < BLOCK:
                            build_onehot(k + LOOKAHEAD)
                        need(dve, s_add, n * BLOCK + k)
                        if lookup:
                            nc.vector.scalar_tensor_tensor(look_o[:, k % RING, :], iota_f[:, 0:TYPES], type_s[:, k:k + 1],
                                                           alpha_sb[:, :], ALU.is_equal, ALU.mult,
                                                           accum_out=alpha_s[:, k:k + 1]).then_inc(s_look, 1)
                        dve.wait_ge(s_mm, n * BLOCK + (k + 1))
                        window = agg[:, bass.ds(bases[k], WIN)]
                        nc.vector.tensor_tensor(window, window, bank[k % RING][:, 0:WIN], ALU.add).then_inc(s_add, 1)

                def general(j, n):
                    dve.wait_ge(g_open, n + 1)
                    if lookup:
                        need(dve, s_alpha, n)
                    for k in range(BLOCK):
                        for g, (first, size) in enumerate(GROUPS):
                            if k == first:
                                dve.wait_ge(s_place, n * NG + (g + 1))
                        nc.vector.tensor_copy(place_g[:, :], place_s[:, k:k + 1]).then_inc(g_place, 1)
                        if lookup:
                            nc.vector.scalar_tensor_tensor(look_o[:, 0, :], iota_f[:, 0:TYPES], type_s[:, k:k + 1],
                                                           alpha_sb[:, :], ALU.is_equal, ALU.mult,
                                                           accum_out=alpha_s[:, k:k + 1]).then_inc(s_look, 1)
                        with dve.Fori(0, WINS) as w:
                            dve.wait_ge(g_place, w + (k * (WINS + 1) + 1))
                            if layer < 2:
                                nc.vector.tensor_scalar(onehot[:, 0, :], iota_f[:, 0:WIN], place_g[:, 0:1], None,
                                                        ALU.is_equal).then_inc(g_oh, 1)
                            else:
                                nc.vector.tensor_scalar(onehot[:, 0, :], iota_f[:, 0:WIN], place_g[:, 0:1],
                                                        type_s[:, k:k + 1], ALU.is_equal, ALU.mult).then_inc(g_oh, 1)
                            dve.wait_ge(g_mm, w + (k * WINS + 1))
                            nc.vector.tensor_scalar(place_g[:, :], place_g[:, :], float(WIN), None,
                                                    ALU.subtract).then_inc(g_place, 1)
                            nc.vector.tensor_tensor(agg[:, cols(w, WIN)], agg[:, cols(w, WIN)], bank[0][:, 0:WIN], ALU.add)
                        dve.drain().then_inc(s_add, 1)

                with dve.If(out_of_order < 1):
                    over_blocks(dve, layer, step)
                with dve.Else():
                    over_blocks(dve, layer, general)

            out_of_order = dve.value_load(unsorted_i[0:1, 0:1], min_val=0, max_val=1)
            aggregate(0, True)
            dve.wait_ge(s_w2, 48)
            over_tiles(dve, evac(1))
            dve.wait_ge(s_ag, 2 * TILES)
            aggregate(1, True)
            dve.wait_ge(s_alpha, 2 * BLOCKS)
            nc.vector.tensor_tensor(type_t, type_t, rtype_t, ALU.add)
            dve.wait_ge(s_idx, 2 * BLOCKS * NG)
            chain(nc.vector.tensor_copy(index_t.bitcast(i32), index_t))
            nc.vector.tensor_single_scalar(index_t.bitcast(i32), index_t.bitcast(i32), R.bit_length() - 1,
                                           ALU.logical_shift_right).then_inc(s_wgt, 1)

            def residual(t, s):
                tile = x_res[:, bass.ds(t, 1), :].rearrange("p o d -> p (o d)")
                dve.wait_ge(s_rT, t + 1)
                need(dve, s_rx, t)
                nc.vector.tensor_tensor(tile, tile, bank[4 + s][:, 0:P], ALU.add).then_inc(s_rx, 1)
                if not isinstance(t, int) or t > 0:
                    tile_stats(t + (-1))
            over_tiles(dve, residual)
            dve.wait_ge(s_rx, TILES)
            tile_stats(TILES - 1)
            norm_factors(2)
            nc.vector.memset(agg[:, :], 0.0).then_inc(s_dve, 1)
            count[0] += 1
            def add_bias(t, s):
                tile = x_res[:, bass.ds(t, 1), :].rearrange("p o d -> p (o d)")
                dve.wait_ge(s_h2, t + 1)
                nc.vector.tensor_tensor(tile, tile, bias_sb[:, :], ALU.add).then_inc(s_h2b, 1)
            over_tiles(dve, add_bias)
            dve.wait_ge(s_h2b, TILES)
            dve.wait_ge(s_dve, count[0])
            dve.wait_ge(s_wgt, 1)
            aggregate(2, False)

            def final(t, s):
                tile = x_res[:, bass.ds(t, 1), :].rearrange("p o d -> p (o d)")
                dve.wait_ge(s_fm, t + 1)
                nc.vector.tensor_tensor(tile, tile, bank[4 + s][:, 0:P], ALU.add).then_inc(s_fa, 1)
            over_tiles(dve, final)

        @block.tensor
        def _(pe):
            pe.wait_ge(s_desc, 1)
            nc.tensor.matmul(bank[5][:, 0:1], ones[:, :], descent_c[:, :], start=True, stop=True).then_inc(s_desum, 1)
            pe.wait_ge(s_diag, 1)
            nc.tensor.matmul(bank[7][:, 0:WINS], ones[0:WINS, :], start_d[0:WINS, :], start=True, stop=True).then_inc(s_spread, 1)
            pe.wait_ge(s_chunks, 2)
            nc.tensor.transpose(bank[6][0:VT, 0:P], base_v[:, :], ident[:, :]).then_inc(s_baseT, 1)

            pe.wait_ge(s_baser, 1)

            def transpose_tile(t, s):
                pe.wait_ge(s_hn, t + 1)
                need(pe, s_hs, t + (-1))
                nc.tensor.transpose(bank[4 + s][:, 0:P], hn[:, s, :], ident[:, :]).then_inc(s_hT, 1)

            def transform(layer):
                def step(t, s):
                    pe.wait_ge(s_hs, t + (layer * TILES + 1))
                    need(pe, s_eva, t + (layer * TILES - 1))
                    need(pe, s_ag, t + (layer * TILES - 1))
                    for half in range(2):
                        nc.tensor.matmul(bank[2 * s + half][:, 0:HT], hs[:, s, :],
                                         w_sb[:, half * R // 2:(half + 1) * R // 2, :].rearrange("p r d -> p (r d)"),
                                         start=True, stop=True)
                    nc.tensor.matmul(bank[6 + s][:, 0:P], sl_sb[:, :], hs[:, s, :], start=True, stop=True).then_inc(s_xf, 1)
                return step
            pe.wait_ge(s_w, 96)
            lagged(pe, TILES, transpose_tile, transform(0))

            def table_tile(t, s):
                pe.wait_ge(s_conva, t + 1)
                pe.wait_ge(s_convd, t + 1)
                need(pe, s_taba, t + (-1))
                need(pe, s_tabd, t + (-1))
                for a in range(4):
                    last = nc.tensor.transpose(bank[s + a // 2 * 2][:, a % 2 * P:(a % 2 + 1) * P], conv[:, s, a, :], ident[:, :])
                last.then_inc(s_tabT, 1)
            pe.wait_ge(s_eva, TILES)
            pe.wait_ge(s_ag, TILES)
            table_tile(0, 0)
            table_tile(1, 1)
            if VT >= 4:
                with pe.Fori(1, VT // 2) as i:
                    table_tile(i * 2, 0)
                    table_tile(i * 2 + 1, 1)
            if VT % 2:
                table_tile(VT - 1, 0)
            pe.wait_ge(s_taba, VT)
            pe.wait_ge(s_tabd, VT)

            def products(layer):
                def step(j, n):
                    for g, (first, size) in enumerate(GROUPS):
                        pe.wait_ge(s_g[g], n * (16 * size) + 16 * size)
                        for k in range(first, first + size):
                            need(pe, s_add, n * BLOCK + (k - LOOKAHEAD))
                            pe.wait_ge(s_oh, n * BLOCK + (k + 1))
                            nc.tensor.matmul(bank[k % RING][:, 0:WIN], msgs[:, k, :], onehot[:, k % RING, :],
                                             start=True, stop=True).then_inc(s_mm, 1)

                def general(j, n):
                    need(pe, s_add, n * BLOCK)
                    pe.nop(nofuse=True)
                    for s in (g_place, g_oh, g_mm):
                        pe.sem_clear(s)
                    pe.sem_inc(g_open, 1)
                    for g, (first, size) in enumerate(GROUPS):
                        pe.wait_ge(s_g[g], n * (16 * size) + 16 * size)
                        pe.nop(nofuse=True)
                        for k in range(first, first + size):
                            with pe.Fori(0, WINS) as w:
                                pe.wait_ge(g_oh, w + (k * WINS + 1))
                                nc.tensor.matmul(bank[0][:, 0:WIN], msgs[:, k, :], onehot[:, 0, :],
                                                 start=True, stop=True).then_inc(g_mm, 1)
                            pe.drain().then_inc(s_mm, 1)

                with pe.If(out_of_order < 1):
                    over_blocks(pe, layer, step)
                with pe.Else():
                    over_blocks(pe, layer, general)
            pe.wait_ge(s_eva, TILES)
            pe.wait_ge(s_ag, TILES)
            pe.wait_ge(s_flag, 1)
            out_of_order = pe.value_load(unsorted_i[0:1, 0:1], min_val=0, max_val=1)
            products(0)
            pe.wait_ge(s_w2, 48)
            pe.wait_ge(s_add, VISITS)
            over_tiles(pe, transform(1))
            pe.wait_ge(s_eva, 2 * TILES)
            pe.wait_ge(s_ag, 2 * TILES)
            products(1)

            def transpose_relu(t, s):
                pe.wait_ge(s_rl, t + 1)
                need(pe, s_rx, t + (-1))
                nc.tensor.transpose(bank[4 + s][:, 0:P], hs[:, s, :], ident[:, :]).then_inc(s_rT, 1)
            over_tiles(pe, transpose_relu)
            pe.wait_ge(s_rx, TILES)
            products(2)

            def final_product(t, s):
                pe.wait_ge(s_fc, t + 1)
                need(pe, s_fa, t + (-1))
                nc.tensor.matmul(bank[4 + s][:, 0:P], hs[:, s, :], weight_sb[:, :], start=True, stop=True).then_inc(s_fm, 1)
            over_tiles(pe, final_product)


_INS = ["x", "src", "dst", "edge_type_201", "edge_type_8", "L0_gnn_w1", "L0_gnn_sl1", "L0_gnn_b1", "L0_gnn_w2",
        "L0_gnn_sl2", "L0_gnn_b2", "L1_gnn_weight", "L1_gnn_alpha", "L1_gnn_bias"]


def kernel(**inputs):
    import numpy as _np
    import concourse.bacc as _bacc
    from concourse import mybir as _mybir
    from concourse.bass_utils import run_bass_kernel_spmd as _run

    nc = _bacc.Bacc("TRN2", target_bir_lowering=False, num_devices=1)
    arrays, args = {}, []
    for name in _INS:
        a = _np.ascontiguousarray(inputs[name])
        arrays[f"in_{name}_dram"] = a
        args.append(nc.dram_tensor(f"in_{name}_dram", a.shape, _mybir.dt.from_np(a.dtype), kind="ExternalInput").ap())
    args.append(nc.dram_tensor("out_0_dram", inputs["x"].shape, _mybir.dt.float32, kind="ExternalOutput").ap())
    build(nc, *args)
    r = _run(nc, [arrays], core_ids=[0])
    return r.results[0]["out_0_dram"]
```

```python
from contextlib import ExitStack

import concourse.bass as bass
from concourse import mybir

P = 128
WIN = 256
BLOCK = 19
LOOKAHEAD = 2
RING = 4
EPS = 1e-5
REST = 3
FAR = 1 << 20


def split(n, most=8192):
    for unit in (16, 10, 5, 2, 1):
        for rows in range(unit, n + 1, unit):
            if n % rows == 0 and n // rows <= most:
                return rows, n // rows


def build(nc, x, src, dst, etype, rel, w1, sl1, b1, w2, sl2, b2, weight, alpha, bias, out):
    fp32, i32, i16 = mybir.dt.float32, mybir.dt.int32, mybir.dt.int16
    ALU = mybir.AluOpType
    ACT = mybir.ActivationFunctionType

    NODES, D = x.shape
    EDGES = src.shape[0]
    R = w1.shape[0]
    TYPES = alpha.shape[0]
    TILES = -(-NODES // P)
    TAIL = NODES - (TILES - 1) * P
    CHUNKS = EDGES // P
    WINS = -(-NODES // WIN)
    VISITS = -(-(CHUNKS + WINS - 1) // BLOCK) * BLOCK
    BLOCKS = VISITS // BLOCK
    VT = -(-VISITS // P)
    HALF = (EDGES - NODES) // 2
    COLS = TILES * P
    assert TILES % 2 == 0 and TILES >= 4 and D == P and EDGES % P == 0 and VT >= 3 and WINS * WIN >= NODES
    GROUPS = [(g, min(5, BLOCK - g)) for g in range(0, BLOCK, 5)]
    NG = len(GROUPS)
    STEP_AT = [BLOCK // 3, BLOCK // 3 + 1, BLOCK // 3 + 2, BLOCK // 3 + 3, BLOCK - 2, BLOCK - 1]
    STEPS = len(STEP_AT)
    LATE = GROUPS[-1][0]
    FOLLOW = [BLOCK // 5, BLOCK // 2]
    LR = max(r for r in range(1, P + 1) if CHUNKS % r == 0)
    LC = CHUNKS // LR
    TAB = R * D
    HT = TAB // 2

    xt1 = nc.dram_tensor("xt1", (COLS * R, D), fp32, kind="Internal").ap()
    xt2 = nc.dram_tensor("xt2", ((COLS + P) * R, D), fp32, kind="Internal").ap()
    h2_d = nc.dram_tensor("h2_d", (COLS + P, D), fp32, kind="Internal").ap()
    row_d = nc.dram_tensor("row_d", (EDGES,), i32, kind="Internal").ap()
    tet_d = nc.dram_tensor("tet_d", (EDGES,), i32, kind="Internal").ap()
    last_d = nc.dram_tensor("last_d", (CHUNKS,), i32, kind="Internal").ap()
    base_d = nc.dram_tensor("base_d", (VT * P,), i32, kind="Internal").ap()

    with ExitStack() as ctx:
        def sb(name, shape, dt=fp32):
            return ctx.enter_context(nc.sbuf_tensor(name, shape, dt))

        def sem(name):
            return ctx.enter_context(nc.semaphore(name))

        x_res = sb("x_res", [P, TILES + 1, D])
        agg = sb("agg", [P, COLS + P])
        tables = sb("tables", [P, 4, VT * P])
        place_t, index_t, type_t, rtype_t = (tables[:, a, :] for a in range(4))
        base_t = sb("base_t", [1, VT * P], i32)
        iota_i = sb("iota_i", [P, max(WIN, TYPES)], i32)
        iota_f = sb("iota_f", [P, max(WIN, TYPES)])
        row_i = sb("row_i", [P, 1], i32)
        row_f = sb("row_f", [P, 1])
        visit_i = sb("visit_i", [P, VT], i32)
        visit_f = sb("visit_f", [P, VT])
        win_first = sb("win_first", [P, 1])
        ident = sb("ident", [P, P])
        ones = sb("ones", [P, P])
        eps_c = sb("eps_c", [P, 1])
        w_sb = sb("w_sb", [P, R, D])
        sl_sb = sb("sl_sb", [P, D])
        b_col = sb("b_col", [P, 1])
        weight_sb = sb("weight_sb", [P, D])
        bias_sb = sb("bias_sb", [P, D])
        alpha_sb = sb("alpha_sb", [P, TYPES])
        last_sb = sb("last_sb", [P, LC], i32)
        start_c = sb("start_c", [P, 1])
        start_v = sb("start_v", [P, 1])
        start_d = sb("start_d", [P, WINS])
        start_b = sb("start_b", [P, WINS])
        win_v = sb("win_v", [P, VT])
        chunk_v = sb("chunk_v", [P, VT])
        chunk_i = sb("chunk_i", [P, VT], i32)
        first_v = sb("first_v", [P, VT])
        base_v = sb("base_v", [P, VT])
        base_r = sb("base_r", [P, P], i32)
        descent_c = sb("descent_c", [P, 1])
        unsorted = sb("unsorted", [P, 1])
        unsorted_far = sb("unsorted_far", [P, 1])
        unsorted_i = sb("unsorted_i", [P, 1], i32)
        step_v = sb("step_v", [P, 1])
        place_g = sb("place_g", [P, 1])
        stats = sb("stats", [P, TILES, 6])
        mean = sb("mean", [P, TILES])
        gap = sb("gap", [P, TILES])
        var = sb("var", [P, TILES])
        std = sb("std", [P, TILES])
        rstd = sb("rstd", [P, TILES])
        nmr = sb("nmr", [P, TILES])
        hn = sb("hn", [P, 2, P])
        hs = sb("hs", [P, 2, P])
        xts = sb("xts", [P, 2, TAB])
        sorted_1 = sb("sorted_1", [1, 1])
        tile_r = sb("tile_r", [1, BLOCKS + TILES], i32)
        many_f = sb("many_f", [1, 1])
        many_i = sb("many_i", [1, 1], i32)
        hq = sb("hq", [P, P])
        sum_q = sb("sum_q", [P, D])
        stats_q = sb("stats_q", [P, 6])
        mv_q = sb("mv_q", [P, 2])
        std_q = sb("std_q", [P, 1])
        rstd_q = sb("rstd_q", [P, 1])
        nmr_q = sb("nmr_q", [P, 1])
        index_s = sb("index_s", [P, BLOCK], i32)
        msgs = sb("msgs", [P, BLOCK, D])
        conv = msgs[:, 0:8, :].rearrange("p (s a) e -> p s a e", s=2)
        spare = msgs[0:1, 8:BLOCK, :].rearrange("o k d -> o (k d)")
        row_at = [sum([0, BLOCKS, BLOCKS, BLOCKS, BLOCKS + 1, BLOCKS + TILES][:n + 1]) for n in range(6)]
        one_row, final_r, none_r, next_r, tile_f = (spare[:, a:b] for a, b in zip(row_at, row_at[1:]))
        assert row_at[-1] <= (BLOCK - 8) * D
        onehot = sb("onehot", [P, RING, WIN])
        place_s = sb("place_s", [P, BLOCK])
        type_s = sb("type_s", [P, BLOCK])
        alpha_s = sb("alpha_s", [P, BLOCK])
        look_o = sb("look_o", [P, RING, TYPES])
        bank = [ctx.enter_context(nc.psum_tensor(f"bank{i}", [P, 512], fp32)) for i in range(8)]

        last_b = index_t[0:WINS, 0:CHUNKS].bitcast(i32)
        last_f = place_t[0:WINS, 0:CHUNKS]
        below_o = type_t[0:WINS, 0:CHUNKS]

        here = agg[:, 0:CHUNKS].bitcast(i32)
        after = agg[:, CHUNKS:2 * CHUNKS].bitcast(i32)
        descends = agg[:, 0:CHUNKS]
        source_e = index_t[:, 0:CHUNKS].bitcast(i32)
        rel_e = rtype_t[:, 0:CHUNKS].bitcast(i32)
        reached = type_t[:, 0:VT * (WINS - 1)].rearrange("p (t w) -> p t w", w=WINS - 1)
        assert WINS <= P and 2 * CHUNKS <= COLS and EDGES == P * CHUNKS

        s_end = sem("end_of_destinations_set")
        s_pairs = sem("destination_pairs_loaded")
        s_x = [sem(f"x_quarter_{q}_loaded") for q in range(4)]
        s_xtail = sem("x_last_tile_loaded")
        s_dst = sem("last_destinations_loaded")
        s_last = sem("last_destinations_stored")
        s_lastb = sem("last_destinations_broadcast")
        s_tet = sem("reverse_types_stored")
        s_w = sem("weights_loaded")
        s_w2 = sem("second_weights_loaded")
        s_zero = sem("tail_tile_cleared")
        s_iota = sem("iotas_written")
        s_const = sem("constants_written")
        s_dve = sem("vector_step_done")
        s_desc = sem("descents_counted")
        s_desum = sem("descents_summed")
        s_flag = sem("order_flag_ready")
        s_diag = sem("window_starts_on_diagonal")
        s_spread = sem("window_starts_broadcast")
        s_chunks = sem("visit_chunks_written")
        s_baseT = sem("bases_transposed")
        s_baser = sem("base_rows_written")
        s_based = sem("bases_stored")
        s_base = sem("bases_loaded")
        s_edges = sem("sources_and_relations_loaded")
        s_row = sem("edge_rows_computed")
        s_rowd = sem("edge_rows_stored")
        s_raw = sem("table_rows_gathered")
        s_conva = sem("rows_and_types_converted")
        s_convd = sem("places_converted")
        s_tabT = sem("table_transposed")
        s_taba = sem("places_and_rows_in_table")
        s_tabd = sem("types_in_table")
        s_bn = sem("tile_stats_done")
        s_var = sem("variances_ready")
        s_std = sem("std_ready")
        s_norm = sem("norm_factors_ready")
        s_hn = sem("normed_tile_ready")
        s_hT = sem("normed_tile_transposed")
        s_hs = sem("stationary_tile_ready")
        s_xf = sem("tile_transformed")
        s_eva = sem("left_half_evacuated")
        s_evd = sem("right_half_evacuated")
        s_ag = sem("self_term_in_agg")
        s_xts = [sem("tile_rows_stored_0"), sem("tile_rows_stored_1")]
        s_idx = sem("index_group_ready")
        s_g = [sem(f"group_gathered_{g}") for g in range(NG)]
        s_oh = sem("onehot_ready")
        s_mm = sem("product_done")
        s_add = sem("product_added")
        s_place = sem("places_and_types_ready")
        s_look = sem("alpha_looked_up")
        s_alpha = [sem("early_alphas_kept"), sem("late_alphas_kept")]
        g_open = sem("general_block_open")
        g_place = sem("general_place_ready")
        g_oh = sem("general_onehot_ready")
        g_mm = sem("general_product_done")
        s_wgt = sem("edge_weights_ready")
        s_order = sem("follow_order_ready")
        f_in = sem("follow_tile_ready")
        f_mm = sem("follow_half_multiplied")
        f_out = sem("follow_half_evacuated")
        f_stored = sem("follow_rows_stored")
        s_rows2 = sem("second_table_whole")
        s_win = sem("relu_window_ready")
        s_wm = sem("self_window_multiplied")
        s_wa = sem("self_window_in_agg")
        e_in = sem("residual_tile_ready")
        e_T = sem("residual_tile_transposed")
        e_step = sem("residual_step_done")
        e_std = sem("residual_std_ready")
        e_h = sem("residual_tile_normed")
        e_stored = sem("residual_tile_stored")
        s_rows3 = sem("third_table_whole")
        o_in = sem("final_tile_ready")
        o_mm = sem("final_tile_multiplied")
        o_add = sem("final_tile_added")
        s_final = sem("residual_final")
        s_out = sem("output_stored")

        block = ctx.enter_context(nc.Block())

        def need(eng, s, value):
            if not isinstance(value, int) or value > 0:
                eng.wait_ge(s, value)

        def over_tiles(eng, step):
            step(0, 0)
            step(1, 1)
            with eng.Fori(1, TILES // 2) as i:
                step(i * 2, 0)
                step(i * 2 + 1, 1)

        def lagged(eng, tiles, ahead, behind, aside=None):
            ahead(0, 0)
            ahead(1, 1)
            behind(0, 0)
            ahead(2, 0)
            behind(1, 1)
            turns = (tiles - 3) // 2
            pause = 1 + turns // 8 if aside else 1
            for part, (a, b) in enumerate(((1, pause), (pause, turns + 1))):
                if part and aside:
                    aside()
                if b > a:
                    with eng.Fori(a, b) as i:
                        ahead(i * 2 + 1, 1)
                        behind(i * 2, 0)
                        ahead(i * 2 + 2, 0)
                        behind(i * 2 + 1, 1)
            for t in range(2 * turns + 2, tiles):
                if t + 1 < tiles:
                    ahead(t + 1, (t + 1) % 2)
                behind(t, t % 2)

        def over_windows(eng, step):
            step(0, 0)
            step(1, 1)
            if WINS >= 4:
                with eng.Fori(1, WINS // 2) as i:
                    step(i * 2, 0)
                    step(i * 2 + 1, 1)
            if WINS % 2:
                step(WINS - 1, 0)

        def follow_rest(eng, many, step, finish=lambda count: None):
            def turns(count):
                with eng.Fori(BLOCKS, BLOCKS + count) as j:
                    step(j)
                finish(count)
            with eng.If(many < 1):
                turns(REST)
            with eng.Else():
                turns(TILES)

        def over_blocks(eng, layer, step):
            step(0, layer * BLOCKS)
            with eng.Fori(1, BLOCKS) as j:
                step(j, j + layer * BLOCKS)

        quarters = [((TILES - 1) * q // 4, (TILES - 1) * (q + 1) // 4) for q in range(4)]

        def cols(t, width=P):
            return bass.ds(t * width, width)

        def half16(t, s):
            return t * 8 + (-8 * s)

        def stored(eng, t, s):
            eng.wait_ge(s_xts[s], half16(t, s))

        @block.sync
        def _(sp):
            sp.dma_start(here, dst.rearrange("(p c) -> p c", p=P)).then_inc(s_pairs, 16)
            sp.wait_ge(s_end, 1)
            sp.dma_start(after[0:P - 1, :], dst[1:1 + (P - 1) * CHUNKS].rearrange("(p c) -> p c", c=CHUNKS)).then_inc(s_pairs, 16)
            sp.dma_start(after[P - 1:P, 0:CHUNKS - 1],
                         dst[1 + (P - 1) * CHUNKS:EDGES].rearrange("(o c) -> o c", o=1)).then_inc(s_pairs, 16)
            sp.wait_ge(s_zero, 1)
            sp.dma_start(x_res[0:TAIL, TILES - 1, :], x[(TILES - 1) * P:NODES, :]).then_inc(s_xtail, 16)
            for q, (a, b) in enumerate(quarters):
                sp.dma_start(x_res[:, a:b, :], x[a * P:b * P, :].rearrange("(t p) d -> p t d", p=P)).then_inc(s_x[q], 16)
            sp.dma_start(w_sb[:, :, :], w1.rearrange("r d e -> d r e")).then_inc(s_w, 16)
            sp.dma_start(sl_sb[:, :], sl1).then_inc(s_w, 16)
            sp.dma_start(weight_sb[:, :], weight).then_inc(s_w, 16)
            with nc.allow_non_contiguous_dma("biases as columns"):
                sp.dma_start(b_col[:, :], b1.rearrange("(d o) -> d o", o=1)).then_inc(s_w, 16)
                sp.dma_start(bias_sb[:, :], bias.partition_broadcast(P)).then_inc(s_w, 16)
                sp.dma_start(alpha_sb[:, :], alpha.rearrange("r o -> (r o)").partition_broadcast(P)).then_inc(s_w, 16)
            sp.wait_ge(s_diag, 1)
            sp.dma_start(source_e, src.rearrange("(p c) -> p c", p=P)).then_inc(s_edges, 16)
            sp.dma_start(rel_e, rel.rearrange("(p c) -> p c", p=P)).then_inc(s_edges, 16)
            for to, frm, n in ((0, HALF, HALF), (HALF, 0, HALF), (2 * HALF, 2 * HALF, NODES)):
                a, _b = split(n)
                sp.dma_start(tet_d[to:to + n].rearrange("(a b) -> a b", a=a),
                             etype[frm:frm + n].rearrange("(a b) -> a b", a=a)).then_inc(s_tet, 16)
            def store_rows(layer, table):
                def step(t, s):
                    done = t + (layer * TILES + 1)
                    need(sp, s_eva, done)
                    need(sp, s_evd, done)
                    rows = table.rearrange("(n r) d -> n (r d)", r=R)
                    sp.dma_start(rows[cols(t), :], xts[:, s, :]).then_inc(s_xts[s], 16)
                over_tiles(sp, step)

            store_rows(0, xt1)
            sp.wait_ge(s_xf, TILES)
            sp.wait_ge(s_ag, TILES)
            sp.dma_start(w_sb[:, :, :], w2.rearrange("r d e -> d r e")).then_inc(s_w2, 16)
            sp.dma_start(sl_sb[:, :], sl2).then_inc(s_w2, 16)
            with nc.allow_non_contiguous_dma("biases as columns"):
                sp.dma_start(b_col[:, :], b2.rearrange("(d o) -> d o", o=1)).then_inc(s_w2, 16)
            sp.wait_ge(s_order, 1)

            def store_follow(j):
                tile = sp.value_load(tile_r[0:1, bass.ds(j, 1)], min_val=0, max_val=TILES)
                first = sp.snap(tile * P)
                sp.wait_ge(f_out, j * 2 + 2)
                rows = xt2.rearrange("(n r) d -> n (r d)", r=R)
                sp.dma_start(rows[bass.ds(first, P), :], xts[:, 0, :]).then_inc(f_stored, 16)
            with sp.Fori(0, BLOCKS) as j:
                store_follow(j)
            follow_rest(sp, sp.value_load(many_i[0:1, 0:1], min_val=0, max_val=1), store_follow,
                        lambda count: sp.wait_ge(f_stored, 16 * (BLOCKS + count)))
            sp.sem_inc(s_rows2, 1)

            def store_normed(j):
                tile = sp.value_load(tile_r[0:1, bass.ds(j, 1)], min_val=0, max_val=TILES)
                first = sp.snap(tile * P)
                sp.wait_ge(e_h, j + 1)
                sp.dma_start(h2_d[bass.ds(first, P), :], hn[:, 0, :]).then_inc(e_stored, 16)
            with sp.Fori(0, BLOCKS) as j:
                store_normed(j)
            follow_rest(sp, sp.value_load(many_i[0:1, 0:1], min_val=0, max_val=1), store_normed,
                        lambda count: sp.wait_ge(e_stored, 16 * (BLOCKS + count)))
            sp.sem_inc(s_rows3, 1)

            sp.wait_ge(s_final, 1)
            for a, b in quarters:
                sp.dma_start(out[a * P:b * P, :].rearrange("(t p) d -> p t d", p=P), x_res[:, a:b, :]).then_inc(s_out, 16)
            sp.dma_start(out[(TILES - 1) * P:NODES, :], x_res[0:TAIL, TILES - 1, :]).then_inc(s_out, 16)
            sp.wait_ge(s_out, 80)

        @block.gpsimd
        def _(pool):
            nc.gpsimd.iota(iota_i[:, :], pattern=[[1, max(WIN, TYPES)]], base=0, channel_multiplier=0).then_inc(s_iota, 1)
            nc.gpsimd.iota(row_i[:, :], pattern=[[0, 1]], base=0, channel_multiplier=1).then_inc(s_iota, 1)
            nc.gpsimd.iota(visit_i[:, :], pattern=[[P, VT]], base=0, channel_multiplier=1).then_inc(s_iota, 1)

            pool.wait_ge(s_baser, 1)
            pool.dma_start(base_d.rearrange("(t p) -> t p", p=P), base_r[0:VT, :]).then_inc(s_based, 16)
            pool.wait_ge(s_based, 16)
            pool.dma_start(base_t[:, :], base_d.rearrange("(o n) -> o n", o=1)).then_inc(s_base, 16)
            pool.wait_ge(s_row, 1)
            pool.dma_start(row_d.rearrange("(p c) -> p c", p=P), source_e).then_inc(s_rowd, 16)

            arrays = [a.rearrange("(c p) -> c p", p=P) for a in (dst, row_d, etype, tet_d)]
            pool.wait_ge(s_tet, 48)
            pool.wait_ge(s_rowd, 16)

            pool.wait_ge(s_chunks, 1)
            for t in range(VT):
                for a in range(4):
                    pool.indirect_dma_start(out=tables[:, a, t * P:(t + 1) * P].bitcast(i32), out_offset=None, in_=arrays[a],
                                            in_offset=bass.IndirectOffsetOnAxis(ap=chunk_i[:, t:t + 1], axis=0)
                                            ).then_inc(s_raw, 16)

            def gather_layer(layer, table):
                def step(j, n):
                    for g, (first, size) in enumerate(GROUPS):
                        pool.wait_ge(s_idx, n * NG + (g + 1))
                        need(pool, s_mm, n * BLOCK + (first + size - BLOCK))
                        pool.nop(nofuse=True)
                        for k in range(first, first + size):
                            pool.indirect_dma_start(out=msgs[:, k, :], out_offset=None, in_=table,
                                                    in_offset=bass.IndirectOffsetOnAxis(ap=index_s[:, k:k + 1], axis=0)
                                                    ).then_inc(s_g[g], 16)
                over_blocks(pool, layer, step)

            for s in range(2):
                pool.wait_ge(s_xts[s], 8 * TILES)
            gather_layer(0, xt1)
            pool.wait_ge(s_rows2, 1)
            gather_layer(1, xt2)
            pool.wait_ge(s_rows3, 1)
            gather_layer(2, h2_d)

        @block.scalar
        def _(act):
            with nc.allow_non_contiguous_dma("last destination of each chunk: one column"):
                act.dma_start(last_sb[0:LR, 0:LC],
                              dst.rearrange("(a b p) -> a b p", a=LR, p=P)[:, :, P - 1]).then_inc(s_dst, 16)
            act.wait_ge(s_dst, 16)
            act.dma_start(last_d.rearrange("(a b) -> a b", a=LR), last_sb[0:LR, 0:LC]).then_inc(s_last, 16)
            act.wait_ge(s_last, 16)
            act.dma_start(last_b, last_d.partition_broadcast(WINS)).then_inc(s_lastb, 16)

            act.wait_ge(s_var, 1)
            act.wait_ge(s_const, 1)
            nc.scalar.activation(std[:, :], var[:, :], ACT.Sqrt, bias=eps_c[:, 0:1]).then_inc(s_std, 1)
            act.wait_ge(s_norm, 1)

            def norm_tile(t, s):
                need(act, s_hT, t + (-1))
                nc.scalar.activation(hn[:, s, :], x_res[:, bass.ds(t, 1), :].rearrange("p o d -> p (o d)"), ACT.Relu,
                                     bias=nmr[:, bass.ds(t, 1)], scale=rstd[:, bass.ds(t, 1)]).then_inc(s_hn, 1)

            def evac():
                def step(t, s):
                    act.wait_ge(s_xf, t + 1)
                    if not isinstance(t, int) or t >= 2:
                        stored(act, t, s)
                    nc.scalar.copy(xts[:, s, 0:HT], bank[2 * s][:, 0:HT]).then_inc(s_eva, 1)
                return step

            evac_first = evac()
            norm_tile(0, 0)
            norm_tile(1, 1)
            for t in range(2):
                norm_tile(t + 2, t % 2)
                evac_first(t, t % 2)
            with act.Fori(1, TILES // 2 - 1) as i:
                norm_tile(i * 2 + 2, 0)
                evac_first(i * 2, 0)
                norm_tile(i * 2 + 3, 1)
                evac_first(i * 2 + 1, 1)
            evac_first(TILES - 2, 0)
            evac_first(TILES - 1, 1)

            act.wait_ge(s_raw, VT * 64)

            def convert_rest(t, s):
                need(act, s_tabT, t + (-1))
                nc.scalar.copy(conv[:, s, 1:4, :], tables[:, 1:4, cols(t)].bitcast(i32)).then_inc(s_conva, 1)

            def left_tables(t, s):
                act.wait_ge(s_tabT, t + 1)
                act.wait_ge(s_convd, t + 1)
                nc.scalar.copy(tables[:, 0:2, cols(t)],
                               bank[s][:, 0:2 * P].rearrange("p (a e) -> p a e", a=2)).then_inc(s_taba, 1)
            lagged(act, VT, convert_rest, left_tables)

            def follow_in(j):
                tile = act.value_load(tile_r[0:1, bass.ds(j, 1)], min_val=0, max_val=TILES)
                need(act, f_mm, j * 2)
                nc.scalar.activation(hq[:, :], agg[:, bass.ds(tile * P, P)], ACT.Relu).then_inc(f_in, 1)

            def follow_out(j, half):
                if half == 0:
                    need(act, f_stored, j * 16)
                act.wait_ge(f_mm, j * 2 + (half + 1))
                nc.scalar.copy(xts[:, 0, half * HT:(half + 1) * HT], bank[4 + half][:, 0:HT]).then_inc(f_out, 1)

            def residual_in(j):
                tile = act.value_load(tile_r[0:1, bass.ds(j, 1)], min_val=0, max_val=TILES)
                need(act, e_T, j)
                nc.scalar.activation(hq[:, :], agg[:, bass.ds(tile * P, P)], ACT.Relu).then_inc(e_in, 1)

            def residual_std(j):
                act.wait_ge(e_step, j * STEPS + 4)
                nc.scalar.activation(std_q[:, :], mv_q[:, 1:2], ACT.Sqrt, bias=eps_c[:, 0:1]).then_inc(e_std, 1)

            def residual_norm(j):
                need(act, e_stored, j * 16)
                act.wait_ge(e_step, j * STEPS + STEPS)
                nc.scalar.activation(hn[:, 0, :], sum_q[:, :], ACT.Relu, bias=nmr_q[:, 0:1],
                                     scale=rstd_q[:, 0:1]).then_inc(e_h, 1)

            def final_in(j):
                tile = act.value_load(tile_r[0:1, bass.ds(j, 1)], min_val=0, max_val=TILES)
                need(act, o_mm, j)
                nc.scalar.copy(hq[:, :], agg[:, bass.ds(tile * P, P)]).then_inc(o_in, 1)

            def indices(layer, types=None):
                def keep(j, n, late):
                    a, b = (LATE, BLOCK) if late else (0, LATE)
                    act.wait_ge(s_look, n * BLOCK + b)
                    nc.scalar.copy(types[:, bass.ds(j * BLOCK + a, b - a)], alpha_s[:, a:b]).then_inc(s_alpha[late], 1)

                def step(j, n):
                    for g, (first, size) in enumerate(GROUPS):
                        slots = slice(first, first + size)
                        columns = bass.ds(j * BLOCK + first, size)
                        need(act, s_g[g], n * (16 * size))
                        nc.scalar.copy(index_s[:, slots], (index_t if layer < 2 else index_t.bitcast(i32))[:, columns]
                                       ).then_inc(s_idx, 1)
                        need(act, s_add, n * BLOCK + (first + size - BLOCK))
                        nc.scalar.copy(place_s[:, slots], place_t[:, columns])
                        nc.scalar.copy(type_s[:, slots], (type_t if types is None else types)[:, columns]).then_inc(s_place, 1)
                        if layer == 0 and g >= NG - 2 and not (isinstance(j, int) and j == 0):
                            follow_out(j + (-1), g - (NG - 2))
                        if g >= NG - 2 and types is not None and not (isinstance(j, int) and j == 0):
                            keep(j + (-1), n + (-1), g - (NG - 2))
                        if layer == 1 and g >= NG - 2 and not (isinstance(j, int) and j == 0):
                            (residual_std if g == NG - 2 else residual_norm)(j + (-1))
                    if layer == 0:
                        follow_in(j)
                    if layer == 1:
                        residual_in(j)
                    if layer == 2:
                        final_in(j)
                over_blocks(act, layer, step)
                if layer == 1:
                    residual_std(BLOCKS - 1)
                if types is not None:
                    for late in range(2):
                        keep(BLOCKS - 1, (layer + 1) * BLOCKS - 1, late)

            act.wait_ge(s_tabd, VT)
            act.wait_ge(s_order, 1)
            indices(0, type_t)
            act.wait_ge(s_add, VISITS)
            follow_out(BLOCKS - 1, 0)
            follow_out(BLOCKS - 1, 1)

            def rest(j):
                follow_in(j)
                follow_out(j, 0)
                follow_out(j, 1)
            follow_rest(act, act.value_load(many_i[0:1, 0:1], min_val=0, max_val=1), rest)

            def relu_window(w, s):
                nc.scalar.activation(agg[:, cols(w, WIN)], agg[:, cols(w, WIN)], ACT.Relu).then_inc(s_win, 1)
            over_windows(act, relu_window)
            indices(1, rtype_t)

            act.wait_ge(s_add, 2 * VISITS)
            residual_norm(BLOCKS - 1)

            def rest(j):
                residual_in(j)
                residual_std(j)
                residual_norm(j)
            follow_rest(act, act.value_load(many_i[0:1, 0:1], min_val=0, max_val=1), rest)
            act.wait_ge(s_wgt, 1)
            indices(2)

            act.wait_ge(s_add, 3 * VISITS)

            follow_rest(act, act.value_load(many_i[0:1, 0:1], min_val=0, max_val=1), final_in)

        @block.vector
        def _(dve):
            count = [0]

            def chain(ins):
                count[0] += 1
                ins.then_inc(s_dve, 1)
                dve.wait_ge(s_dve, count[0])

            nc.vector.memset(x_res[:, TILES - 1:TILES + 1, :], 0.0).then_inc(s_zero, 1)
            nc.vector.memset(after[:, CHUNKS - 1:CHUNKS], FAR).then_inc(s_end, 1)
            nc.vector.memset(ones[:, :], 1.0)
            dve.wait_ge(s_iota, 3)
            nc.vector.tensor_copy(iota_f[:, :], iota_i[:, :])
            nc.vector.tensor_copy(visit_f[:, :], visit_i[:, :])
            chain(nc.vector.tensor_copy(row_f[:, :], row_i[:, :]))
            nc.vector.tensor_scalar(win_first[:, :], row_f[:, :], float(WIN), None, ALU.mult)
            chain(nc.vector.tensor_scalar(ident[:, :], iota_f[:, 0:P], row_f[:, 0:1], None, ALU.is_equal))
            nc.vector.memset(eps_c[:, :], EPS).then_inc(s_const, 1)

            dve.wait_ge(s_pairs, 48)
            chain(nc.vector.tensor_tensor(descends, after, here, ALU.is_lt))
            nc.vector.reduce_sum(descent_c[:, :], descends, mybir.AxisListType.X).then_inc(s_desc, 1)
            dve.wait_ge(s_desum, 1)
            chain(nc.vector.tensor_scalar(unsorted[:, :], bank[5][:, 0:1], 1.0, None, ALU.min))
            chain(nc.vector.tensor_scalar(unsorted_far[:, :], unsorted[:, :], float(FAR), None, ALU.mult))
            nc.vector.tensor_scalar(step_v[:, :], unsorted_far[:, :], float(WIN), None, ALU.add)
            nc.vector.tensor_copy(unsorted_i[:, :], unsorted[:, :]).then_inc(s_flag, 1)

            dve.wait_ge(s_lastb, 16)
            chain(nc.vector.tensor_copy(last_f, last_b))
            chain(nc.vector.tensor_scalar(below_o, last_f, win_first[0:WINS, 0:1], None, ALU.is_lt, ALU.add,
                                          accum_out=start_c[0:WINS, 0:1]))
            chain(nc.vector.tensor_tensor(start_v[0:WINS, :], start_c[0:WINS, :], row_f[0:WINS, :], ALU.add))
            chain(nc.vector.tensor_tensor(start_v[0:WINS, :], start_v[0:WINS, :], unsorted_far[0:WINS, :], ALU.add))
            nc.vector.tensor_scalar(start_d[0:WINS, :], ident[0:WINS, 0:WINS], start_v[0:WINS, 0:1], None,
                                    ALU.mult).then_inc(s_diag, 1)
            dve.wait_ge(s_spread, 1)
            chain(nc.vector.tensor_copy(start_b[:, :], bank[7][:, 0:WINS]))
            shape = [P, VT, WINS - 1]
            chain(nc.vector.tensor_tensor(reached, start_b[:, 1:WINS].unsqueeze(1).to_broadcast(shape),
                                          visit_f[:, :].unsqueeze(2).to_broadcast(shape), ALU.is_le))
            chain(nc.vector.reduce_sum(win_v[:, :], reached, mybir.AxisListType.X))
            chain(nc.vector.tensor_tensor(chunk_v[:, :], visit_f[:, :], win_v[:, :], ALU.subtract))
            chain(nc.vector.tensor_scalar(chunk_v[:, :], chunk_v[:, :], float(CHUNKS - 1), None, ALU.min))
            chain(nc.vector.tensor_tensor(first_v[:, :], visit_f[:, :], chunk_v[:, :], ALU.subtract))
            chain(nc.vector.tensor_scalar(first_v[:, :], first_v[:, :], step_v[:, 0:1], None, ALU.mult))
            nc.vector.tensor_copy(chunk_i[:, :], chunk_v[:, :]).then_inc(s_chunks, 1)
            nc.vector.tensor_scalar(base_v[:, :], first_v[:, :], float(WIN * (WINS - 1)), None, ALU.min).then_inc(s_chunks, 1)
            dve.wait_ge(s_baseT, 1)
            nc.vector.tensor_copy(base_r[0:VT, :], bank[6][0:VT, 0:P]).then_inc(s_baser, 1)

            def tile_stats(t):
                nc.vector.bn_stats(stats[:, bass.ds(t, 1), :].rearrange("p o d -> p (o d)"),
                                   x_res[:, bass.ds(t, 1), :].rearrange("p o d -> p (o d)")).then_inc(s_bn, 1)

            dve.wait_ge(s_xtail, 16)
            tile_stats(TILES - 1)
            for q, (a, b) in enumerate(quarters):
                dve.wait_ge(s_x[q], 16)
                unroll = min(8, b - a)
                with dve.Fori(0, (b - a) // unroll) as i:
                    for u in range(unroll):
                        tile_stats(i * unroll + (a + u))
                for t in range(a + (b - a) // unroll * unroll, b):
                    tile_stats(t)

            dve.wait_ge(s_bn, TILES)
            nc.vector.tensor_tensor(mean[:, :], stats[:, :, 1], stats[:, :, 4], ALU.add)
            nc.vector.tensor_tensor(gap[:, :], stats[:, :, 1], stats[:, :, 4], ALU.subtract)
            chain(nc.vector.tensor_tensor(var[:, :], stats[:, :, 2], stats[:, :, 5], ALU.add))
            nc.vector.tensor_scalar(mean[:, :], mean[:, :], 0.5, None, ALU.mult)
            chain(nc.vector.tensor_tensor(gap[:, :], gap[:, :], gap[:, :], ALU.mult))
            chain(nc.vector.tensor_scalar(gap[:, :], gap[:, :], 0.25, None, ALU.mult))
            nc.vector.scalar_tensor_tensor(var[:, :], var[:, :], 1.0 / D, gap[:, :], ALU.mult, ALU.add).then_inc(s_var, 1)
            dve.wait_ge(s_std, 1)
            chain(nc.vector.reciprocal(rstd[:, :], std[:, :]))
            nc.vector.scalar_tensor_tensor(nmr[:, :], mean[:, :], -1.0, rstd[:, :], ALU.mult, ALU.mult).then_inc(s_norm, 1)

            def edge_rows():
                dve.wait_ge(s_edges, 32)
                nc.vector.scalar_tensor_tensor(source_e, source_e, float(R), rel_e, ALU.mult, ALU.add).then_inc(s_row, 1)

            def stationary(t, s):
                dve.wait_ge(s_hT, t + 1)
                need(dve, s_xf, t + (-1))
                nc.vector.tensor_copy(hs[:, s, :], bank[4 + s][:, 0:P]).then_inc(s_hs, 1)

            def evac():
                def step(t, s):
                    dve.wait_ge(s_xf, t + 1)
                    if not isinstance(t, int) or t >= 2:
                        stored(dve, t, s)
                    nc.vector.tensor_copy(xts[:, s, HT:TAB], bank[2 * s + 1][:, 0:HT]).then_inc(s_evd, 1)
                    nc.vector.tensor_scalar(agg[:, cols(t)], bank[6 + s][:, 0:P], b_col[:, 0:1], None,
                                            ALU.add).then_inc(s_ag, 1)
                return step
            dve.wait_ge(s_w, 96)
            lagged(dve, TILES, stationary, evac(), aside=edge_rows)

            dve.wait_ge(s_raw, VT * 64)

            def convert_places(t, s):
                need(dve, s_tabT, t + (-1))
                nc.vector.tensor_scalar(conv[:, s, 0, :], place_t[:, cols(t)].bitcast(i32), first_v[:, bass.ds(t, 1)], None,
                                        ALU.subtract).then_inc(s_convd, 1)

            def right_tables(t, s):
                dve.wait_ge(s_tabT, t + 1)
                nc.vector.tensor_copy(tables[:, 2:4, cols(t)],
                                      bank[2 + s][:, 0:2 * P].rearrange("p (a e) -> p a e", a=2)).then_inc(s_tabd, 1)
            lagged(dve, VT, convert_places, right_tables)

            nc.vector.memset(alpha_sb[:, 0:1], 0.0)
            nc.vector.memset(agg[:, COLS:COLS + P], 0.0).then_inc(s_const, 1)
            dve.wait_ge(s_const, 2)
            dve.wait_ge(s_base, 16)
            dve.wait_ge(s_taba, VT)

            chain(nc.vector.tensor_scalar(sorted_1[:, :], unsorted[0:1, :], -1.0, 1.0, ALU.mult, ALU.add))
            chain(nc.vector.tensor_scalar(final_r[:, :], base_t[0:1, 0:VISITS:BLOCK], 1.0 / P, None, ALU.mult))
            nc.vector.memset(next_r[:, 0:1], 0.0)
            chain(nc.vector.memset(one_row[:, :], 1.0))
            chain(nc.vector.tensor_scalar(final_r[:, :], final_r[:, :], sorted_1[:, 0:1], None, ALU.mult))
            chain(nc.vector.tensor_tensor_scan(next_r[:, 1:BLOCKS + 1], one_row[:, :], final_r[:, :], 0.0, ALU.add, ALU.min))
            nc.vector.tensor_scalar(tile_f[:, BLOCKS:BLOCKS + TILES], iota_f[0:1, 0:TILES], next_r[0:1, BLOCKS:BLOCKS + 1],
                                    float(TILES), ALU.add, ALU.min)
            nc.vector.tensor_scalar(many_f[:, :], next_r[0:1, BLOCKS:BLOCKS + 1], float(TILES - REST), None, ALU.is_lt)
            chain(nc.vector.tensor_tensor(none_r[:, :], next_r[:, 0:BLOCKS], final_r[:, :], ALU.is_ge))
            chain(nc.vector.scalar_tensor_tensor(tile_f[:, 0:BLOCKS], none_r[:, :], float(TILES), next_r[:, 0:BLOCKS],
                                                 ALU.mult, ALU.max))
            nc.vector.tensor_copy(many_i[:, :], many_f[:, :])
            nc.vector.tensor_copy(tile_r[:, :], tile_f[:, :]).then_inc(s_order, 1)
            dve.wait_ge(s_ag, TILES)

            def residual_step(j, step, alone):
                if step == 0:
                    tile = dve.value_load(tile_r[0:1, bass.ds(j, 1)], min_val=0, max_val=TILES)
                    tiles_q.append(tile)
                    need(dve, e_h, j)
                    dve.wait_ge(e_T, j + 1)
                elif step == 4:
                    dve.wait_ge(e_std, j + 1)
                elif alone:
                    dve.wait_ge(e_step, j * STEPS + step)
                if alone and step == 2:
                    dve.nop(nofuse=True)
                row = x_res[:, bass.ds(tiles_q[-1], 1), :].rearrange("p o d -> p (o d)")
                ins = [lambda: nc.vector.tensor_tensor(sum_q[:, :], row, bank[4][:, 0:P], ALU.add),
                       lambda: nc.vector.bn_stats(stats_q[:, :], sum_q[:, :]),
                       lambda: nc.vector.bn_aggr(mv_q[:, :], stats_q[:, :]),
                       lambda: nc.vector.tensor_tensor(row, sum_q[:, :], bias_sb[:, :], ALU.add),
                       lambda: nc.vector.reciprocal(rstd_q[:, :], std_q[:, :]),
                       lambda: nc.vector.scalar_tensor_tensor(nmr_q[:, :], mv_q[:, 0:1], -1.0, rstd_q[:, :],
                                                              ALU.mult, ALU.mult)][step]()
                ins.then_inc(e_step, 1)
            tiles_q = []

            def final_step(j):
                tile = dve.value_load(tile_r[0:1, bass.ds(j, 1)], min_val=0, max_val=TILES)
                row = x_res[:, bass.ds(tile, 1), :].rearrange("p o d -> p (o d)")
                dve.wait_ge(o_mm, j + 1)
                nc.vector.tensor_tensor(row, row, bank[4][:, 0:P], ALU.add).then_inc(o_add, 1)

            def aggregate(layer, lookup):
                def step(j, n):
                    bases = []

                    def build_onehot(k):
                        if k in [first for first, _ in GROUPS]:
                            g = [first for first, _ in GROUPS].index(k)
                            dve.wait_ge(s_place, n * NG + (g + 1))
                        if layer < 2:
                            ins = nc.vector.tensor_scalar(onehot[:, k % RING, :], iota_f[:, 0:WIN], place_s[:, k:k + 1], None,
                                                          ALU.is_equal)
                        else:
                            ins = nc.vector.tensor_scalar(onehot[:, k % RING, :], iota_f[:, 0:WIN], place_s[:, k:k + 1],
                                                          type_s[:, k:k + 1], ALU.is_equal, ALU.mult)
                        ins.then_inc(s_oh, 1)
                    for k in range(LOOKAHEAD):
                        build_onehot(k)
                    for k in range(BLOCK):
                        if lookup and k in (0, LATE):
                            need(dve, s_alpha[k == LATE], n)
                        for first, size in GROUPS:
                            if k == first:
                                _, values = nc.values_load_multi_w_load_instructions(
                                    base_t[0:1, bass.ds(j * BLOCK + first, size)], engines=[dve.engine],
                                    min_val=0, max_val=WIN * (WINS - 1),
                                    skip_runtime_bounds_check_because="written with a minimum against the last window's first column")
                                bases.extend(values)
                        if k + LOOKAHEAD < BLOCK:
                            build_onehot(k + LOOKAHEAD)
                        need(dve, s_add, n * BLOCK + k)
                        if lookup:
                            nc.vector.scalar_tensor_tensor(look_o[:, k % RING, :], iota_f[:, 0:TYPES], type_s[:, k:k + 1],
                                                           alpha_sb[:, :], ALU.is_equal, ALU.mult,
                                                           accum_out=alpha_s[:, k:k + 1]).then_inc(s_look, 1)
                        if layer == 1 and k in STEP_AT:
                            residual_step(j, STEP_AT.index(k), False)
                        if layer == 2 and k == STEP_AT[0]:
                            final_step(j)
                        dve.wait_ge(s_mm, n * BLOCK + (k + 1))
                        window = agg[:, bass.ds(bases[k], WIN)]
                        nc.vector.tensor_tensor(window, window, bank[k % RING][:, 0:WIN], ALU.add).then_inc(s_add, 1)

                def general(j, n):
                    dve.wait_ge(g_open, n + 1)
                    for k in range(BLOCK):
                        if lookup and k in (0, LATE):
                            need(dve, s_alpha[k == LATE], n)
                        for g, (first, size) in enumerate(GROUPS):
                            if k == first:
                                dve.wait_ge(s_place, n * NG + (g + 1))
                        nc.vector.tensor_copy(place_g[:, :], place_s[:, k:k + 1]).then_inc(g_place, 1)
                        if lookup:
                            nc.vector.scalar_tensor_tensor(look_o[:, 0, :], iota_f[:, 0:TYPES], type_s[:, k:k + 1],
                                                           alpha_sb[:, :], ALU.is_equal, ALU.mult,
                                                           accum_out=alpha_s[:, k:k + 1]).then_inc(s_look, 1)
                        with dve.Fori(0, WINS) as w:
                            dve.wait_ge(g_place, w + (k * (WINS + 1) + 1))
                            if layer < 2:
                                nc.vector.tensor_scalar(onehot[:, 0, :], iota_f[:, 0:WIN], place_g[:, 0:1], None,
                                                        ALU.is_equal).then_inc(g_oh, 1)
                            else:
                                nc.vector.tensor_scalar(onehot[:, 0, :], iota_f[:, 0:WIN], place_g[:, 0:1],
                                                        type_s[:, k:k + 1], ALU.is_equal, ALU.mult).then_inc(g_oh, 1)
                            dve.wait_ge(g_mm, w + (k * WINS + 1))
                            nc.vector.tensor_scalar(place_g[:, :], place_g[:, :], float(WIN), None,
                                                    ALU.subtract).then_inc(g_place, 1)
                            nc.vector.tensor_tensor(agg[:, cols(w, WIN)], agg[:, cols(w, WIN)], bank[0][:, 0:WIN], ALU.add)
                        dve.drain().then_inc(s_add, 1)
                        if layer == 1 and k in STEP_AT:
                            residual_step(j, STEP_AT.index(k), True)
                        if layer == 2 and k == STEP_AT[0]:
                            final_step(j)

                with dve.If(out_of_order < 1):
                    over_blocks(dve, layer, step)
                with dve.Else():
                    over_blocks(dve, layer, general)

            out_of_order = dve.value_load(unsorted_i[0:1, 0:1], min_val=0, max_val=1)
            aggregate(0, True)
            dve.wait_ge(s_w2, 48)

            def self_term(w, s):
                dve.wait_ge(s_wm, w + 1)
                nc.vector.tensor_scalar(agg[:, cols(w, WIN)], bank[6 + s][:, 0:WIN], b_col[:, 0:1], None,
                                        ALU.add).then_inc(s_wa, 1)
            over_windows(dve, self_term)
            dve.wait_ge(s_wa, WINS)
            aggregate(1, True)
            dve.wait_ge(s_idx, 2 * BLOCKS * NG)
            chain(nc.vector.tensor_copy(index_t.bitcast(i32), index_t))
            chain(nc.vector.tensor_single_scalar(index_t.bitcast(i32), index_t.bitcast(i32), R.bit_length() - 1,
                                                 ALU.logical_shift_right))
            for kept in s_alpha:
                dve.wait_ge(kept, 2 * BLOCKS)
            nc.vector.tensor_tensor(type_t, type_t, rtype_t, ALU.add).then_inc(s_wgt, 1)

            def rest(j):
                for step in range(STEPS):
                    residual_step(j, step, True)
            follow_rest(dve, dve.value_load(many_i[0:1, 0:1], min_val=0, max_val=1), rest)
            chain(nc.vector.memset(agg[:, 0:COLS], 0.0))
            dve.wait_ge(s_wgt, 1)
            aggregate(2, False)

            follow_rest(dve, dve.value_load(many_i[0:1, 0:1], min_val=0, max_val=1), final_step,
                        lambda count: dve.wait_ge(o_add, BLOCKS + count))
            dve.sem_inc(s_final, 1)

        @block.tensor
        def _(pe):
            pe.wait_ge(s_desc, 1)
            nc.tensor.matmul(bank[5][:, 0:1], ones[:, :], descent_c[:, :], start=True, stop=True).then_inc(s_desum, 1)
            pe.wait_ge(s_diag, 1)
            nc.tensor.matmul(bank[7][:, 0:WINS], ones[0:WINS, :], start_d[0:WINS, :], start=True, stop=True).then_inc(s_spread, 1)
            pe.wait_ge(s_chunks, 2)
            nc.tensor.transpose(bank[6][0:VT, 0:P], base_v[:, :], ident[:, :]).then_inc(s_baseT, 1)

            pe.wait_ge(s_baser, 1)

            def transpose_tile(t, s):
                pe.wait_ge(s_hn, t + 1)
                need(pe, s_hs, t + (-1))
                nc.tensor.transpose(bank[4 + s][:, 0:P], hn[:, s, :], ident[:, :]).then_inc(s_hT, 1)

            def transform():
                def step(t, s):
                    pe.wait_ge(s_hs, t + 1)
                    need(pe, s_eva, t + (-1))
                    need(pe, s_ag, t + (-1))
                    for half in range(2):
                        nc.tensor.matmul(bank[2 * s + half][:, 0:HT], hs[:, s, :],
                                         w_sb[:, half * R // 2:(half + 1) * R // 2, :].rearrange("p r d -> p (r d)"),
                                         start=True, stop=True)
                    nc.tensor.matmul(bank[6 + s][:, 0:P], sl_sb[:, :], hs[:, s, :], start=True, stop=True).then_inc(s_xf, 1)
                return step
            pe.wait_ge(s_w, 96)
            lagged(pe, TILES, transpose_tile, transform())

            def table_tile(t, s):
                pe.wait_ge(s_conva, t + 1)
                pe.wait_ge(s_convd, t + 1)
                need(pe, s_taba, t + (-1))
                need(pe, s_tabd, t + (-1))
                for a in range(4):
                    last = nc.tensor.transpose(bank[s + a // 2 * 2][:, a % 2 * P:(a % 2 + 1) * P], conv[:, s, a, :], ident[:, :])
                last.then_inc(s_tabT, 1)
            pe.wait_ge(s_eva, TILES)
            pe.wait_ge(s_ag, TILES)
            table_tile(0, 0)
            table_tile(1, 1)
            if VT >= 4:
                with pe.Fori(1, VT // 2) as i:
                    table_tile(i * 2, 0)
                    table_tile(i * 2 + 1, 1)
            if VT % 2:
                table_tile(VT - 1, 0)
            pe.wait_ge(s_taba, VT)
            pe.wait_ge(s_tabd, VT)

            def follow(j, half):
                pe.wait_ge(f_in, j + 1)
                need(pe, f_out, j * 2 + (half - 1))
                nc.tensor.matmul(bank[4 + half][:, 0:HT], hq[:, :],
                                 w_sb[:, half * R // 2:(half + 1) * R // 2, :].rearrange("p r d -> p (r d)"),
                                 start=True, stop=True).then_inc(f_mm, 1)

            def residual_tile(j):
                pe.wait_ge(e_in, j + 1)
                need(pe, e_step, j * STEPS + (1 - STEPS))
                nc.tensor.transpose(bank[4][:, 0:P], hq[:, :], ident[:, :]).then_inc(e_T, 1)

            def final_product(j):
                pe.wait_ge(o_in, j + 1)
                need(pe, o_add, j)
                nc.tensor.matmul(bank[4][:, 0:P], hq[:, :], weight_sb[:, :], start=True, stop=True).then_inc(o_mm, 1)

            def products(layer):
                def step(j, n):
                    for g, (first, size) in enumerate(GROUPS):
                        pe.wait_ge(s_g[g], n * (16 * size) + 16 * size)
                        for k in range(first, first + size):
                            need(pe, s_add, n * BLOCK + (k - LOOKAHEAD))
                            pe.wait_ge(s_oh, n * BLOCK + (k + 1))
                            nc.tensor.matmul(bank[k % RING][:, 0:WIN], msgs[:, k, :], onehot[:, k % RING, :],
                                             start=True, stop=True).then_inc(s_mm, 1)
                            if layer == 0 and k in FOLLOW:
                                follow(j, FOLLOW.index(k))
                            if layer == 1 and k == FOLLOW[0]:
                                residual_tile(j)
                            if layer == 2 and k == FOLLOW[0]:
                                final_product(j)

                def general(j, n):
                    need(pe, s_add, n * BLOCK)
                    pe.nop(nofuse=True)
                    for s in (g_place, g_oh, g_mm):
                        pe.sem_clear(s)
                    pe.sem_inc(g_open, 1)
                    for g, (first, size) in enumerate(GROUPS):
                        pe.wait_ge(s_g[g], n * (16 * size) + 16 * size)
                        pe.nop(nofuse=True)
                        for k in range(first, first + size):
                            with pe.Fori(0, WINS) as w:
                                pe.wait_ge(g_oh, w + (k * WINS + 1))
                                nc.tensor.matmul(bank[0][:, 0:WIN], msgs[:, k, :], onehot[:, 0, :],
                                                 start=True, stop=True).then_inc(g_mm, 1)
                            pe.drain().then_inc(s_mm, 1)
                            if layer == 0 and k in FOLLOW:
                                follow(j, FOLLOW.index(k))
                            if layer == 1 and k == FOLLOW[0]:
                                residual_tile(j)
                            if layer == 2 and k == FOLLOW[0]:
                                final_product(j)

                with pe.If(out_of_order < 1):
                    over_blocks(pe, layer, step)
                with pe.Else():
                    over_blocks(pe, layer, general)
            pe.wait_ge(s_flag, 1)
            out_of_order = pe.value_load(unsorted_i[0:1, 0:1], min_val=0, max_val=1)
            pe.wait_ge(s_w2, 48)
            products(0)

            def rest(j):
                follow(j, 0)
                follow(j, 1)
            pe.wait_ge(s_order, 1)
            follow_rest(pe, pe.value_load(many_i[0:1, 0:1], min_val=0, max_val=1), rest)

            def self_window(w, s):
                pe.wait_ge(s_win, w + 1)
                need(pe, s_wa, w + (-1))
                nc.tensor.matmul(bank[6 + s][:, 0:WIN], sl_sb[:, :], agg[:, cols(w, WIN)],
                                 start=True, stop=True).then_inc(s_wm, 1)
            over_windows(pe, self_window)
            products(1)

            follow_rest(pe, pe.value_load(many_i[0:1, 0:1], min_val=0, max_val=1), residual_tile)
            products(2)

            follow_rest(pe, pe.value_load(many_i[0:1, 0:1], min_val=0, max_val=1), final_product)


_INS = ["x", "src", "dst", "edge_type_201", "edge_type_8", "L0_gnn_w1", "L0_gnn_sl1", "L0_gnn_b1", "L0_gnn_w2",
        "L0_gnn_sl2", "L0_gnn_b2", "L1_gnn_weight", "L1_gnn_alpha", "L1_gnn_bias"]


def kernel(**inputs):
    import numpy as _np
    import concourse.bacc as _bacc
    from concourse import mybir as _mybir
    from concourse.bass_utils import run_bass_kernel_spmd as _run

    nc = _bacc.Bacc("TRN2", target_bir_lowering=False, num_devices=1)
    arrays, args = {}, []
    for name in _INS:
        a = _np.ascontiguousarray(inputs[name])
        arrays[f"in_{name}_dram"] = a
        args.append(nc.dram_tensor(f"in_{name}_dram", a.shape, _mybir.dt.from_np(a.dtype), kind="ExternalInput").ap())
    args.append(nc.dram_tensor("out_0_dram", inputs["x"].shape, _mybir.dt.float32, kind="ExternalOutput").ap())
    build(nc, *args)
    r = _run(nc, [arrays], core_ids=[0])
    return r.results[0]["out_0_dram"]
```
